# Optimizing a Trainium2 kernel written in Bass

```python
import numpy as np
import jax
import jax.numpy as jnp

def _softmax(x, axis=-1):
    return jax.nn.softmax(x, axis=axis)

def _gelu(x):
    return jax.nn.gelu(x, approximate=True)

def _silu(x):
    return jax.nn.silu(x)

def _sigmoid(x):
    return jax.nn.sigmoid(x)

def _layernorm(x, axis=-1, eps=1e-05):
    m = jnp.mean(x, axis=axis, keepdims=True)
    v = jnp.var(x, axis=axis, keepdims=True)
    return (x - m) / jnp.sqrt(v + eps)

def _scatter_add(tgt, idx, src, axis=0):
    return tgt.at[idx].add(src)

def _segment_sum(src, seg, n):
    return jax.ops.segment_sum(src, seg, n)
kernel_name = 'mk_decoder_postln_d1_seqx_r4_194acb'

def setup_inputs(seed: int=0):
    np.random.seed(seed)
    _w = jnp.asarray

    def _rec_inputs():
        import jax
        import jax.numpy as jnp
        _rk = jax.random.key(seed)
        x = 0.0002417 + 0.9998 * jax.random.normal(jax.random.fold_in(_rk, 1), (16, 256, 256), jnp.float32)
        _lenS = 256 - jax.random.randint(jax.random.fold_in(_rk, 7), (16,), 0, max(1, 256 // 4) + 1, jnp.int32)
        _lenS2 = 120 - jax.random.randint(jax.random.fold_in(_rk, 8), (16,), 0, max(1, 120 // 4) + 1, jnp.int32)
        _ctx_1024P = jax.random.normal(jax.random.fold_in(_rk, 11), (16, 16, 256), jnp.float32)
        _ctx_1024c = jax.random.dirichlet(jax.random.fold_in(_rk, 511), 0.3 * jnp.ones((16,), jnp.float32), (16, 120))
        _ctx_1024t = jnp.einsum('bsk,bkd->bsd', _ctx_1024c, _ctx_1024P)
        _ctx_1024t = _ctx_1024t * jax.lax.rsqrt(jnp.mean(jnp.square(_ctx_1024t)) + 1e-12) * 0.953939
        ctx_1024 = 7.22013e-05 + 1.00017 * (_ctx_1024t + 0.3 * jax.random.normal(jax.random.fold_in(_rk, 611), (16, 120, 256), jnp.float32))
        _validS = jnp.arange(256)[None, :] < _lenS[:, None]
        _validS2 = jnp.arange(120)[None, :] < _lenS2[:, None]
        _causal = jnp.tril(jnp.ones((256, 256), dtype=bool))
        mask_Bx1x1xS2_fk0 = jnp.where(jnp.broadcast_to(_validS2[:, None, None, :], (16, 1, 1, 120)), 0.0, 1.0).astype(jnp.float32)
        return (x, ctx_1024, mask_Bx1x1xS2_fk0)
    x, ctx_1024, mask_Bx1x1xS2_fk0 = _rec_inputs()

    def _L0_attn_setup():
        import jax, jax.numpy as jnp
        import numpy as np
        import math
        NUM_HEADS = 16

        def _alibi_bias(L, num_heads):
            slopes = jnp.power(2.0, jnp.linspace(-4.0, -0.3, num_heads))
            pos = jnp.arange(L, dtype=jnp.float32)
            return -(slopes[:, None] * pos[None, :])
        key = jax.random.key(seed)
        ks = jax.random.split(key, 9)
        B, L, D = (2, 512, 256)
        s = 0.02
        return {'x': jax.random.normal(ks[0], (B, L, D), dtype=jnp.float32), 'Wq': jax.random.normal(ks[1], (D, D), dtype=jnp.float32) * s, 'bq': jax.random.normal(ks[2], (D,), dtype=jnp.float32) * s, 'Wk': jax.random.normal(ks[3], (D, D), dtype=jnp.float32) * s, 'bk': jax.random.normal(ks[4], (D,), dtype=jnp.float32) * s, 'Wv': jax.random.normal(ks[5], (D, D), dtype=jnp.float32) * s, 'bv': jax.random.normal(ks[6], (D,), dtype=jnp.float32) * s, 'Wo': jax.random.normal(ks[7], (D, D), dtype=jnp.float32) * s, 'bo': jax.random.normal(ks[8], (D,), dtype=jnp.float32) * s}
    _L0_attn_all = _L0_attn_setup()
    _L0_attn_in = {k: v for k, v in _L0_attn_all.items() if k in ('Wq', 'bq', 'Wk', 'bk', 'Wv', 'bv', 'Wo', 'bo')}
    del _L0_attn_all

    def _L0_xattn_setup():
        import jax, jax.numpy as jnp
        import numpy as np
        B, S, D, H = (4, 512, 256, 16)
        DEPTH = D // H

        def _split_heads(x):
            b, s, _ = x.shape
            return x.reshape(b, s, H, DEPTH).transpose(0, 2, 1, 3)
        key = jax.random.key(seed)
        ks = jax.random.split(key, 12)
        inp = {'v': jax.random.normal(ks[0], (B, S, D), dtype=jnp.float32), 'k': jax.random.normal(ks[1], (B, S, D), dtype=jnp.float32), 'q': jax.random.normal(ks[2], (B, S, D), dtype=jnp.float32), 'mask': jax.random.randint(ks[3], (B, 1, 1, S), 0, 2).astype(jnp.float32), 'Wq': jax.random.normal(ks[4], (D, D), dtype=jnp.float32) / np.sqrt(D), 'bq': jnp.zeros((D,), dtype=jnp.float32), 'Wk': jax.random.normal(ks[5], (D, D), dtype=jnp.float32) / np.sqrt(D), 'bk': jnp.zeros((D,), dtype=jnp.float32), 'Wv': jax.random.normal(ks[6], (D, D), dtype=jnp.float32) / np.sqrt(D), 'bv': jnp.zeros((D,), dtype=jnp.float32), 'Wo': jax.random.normal(ks[7], (D, D), dtype=jnp.float32) / np.sqrt(D), 'bo': jnp.zeros((D,), dtype=jnp.float32)}
        return inp
    _L0_xattn_all = _L0_xattn_setup()
    _L0_xattn_in = {k: v for k, v in _L0_xattn_all.items() if k in ('Wq', 'bq', 'Wk', 'bk', 'Wv', 'bv', 'Wo', 'bo')}
    del _L0_xattn_all

    def _L0_ffn_setup():
        import jax, jax.numpy as jnp
        import numpy as np
        TEMPERATURE = 1.0
        TOPK = 2
        key = jax.random.key(seed)
        ks = jax.random.split(key, 6)
        S, B, H, F, E = (512, 4, 256, 1024, 8)
        x = jax.random.normal(ks[0], (S, B, H), dtype=jnp.float32)
        gate_w = jax.random.normal(ks[1], (E, H), dtype=jnp.float32) * (1.0 / np.sqrt(H))
        w1 = jax.random.normal(ks[2], (E, H, F), dtype=jnp.float32) * (1.0 / np.sqrt(H))
        b1 = jnp.zeros((E, F), dtype=jnp.float32)
        w2 = jax.random.normal(ks[3], (E, F, H), dtype=jnp.float32) * (1.0 / np.sqrt(F))
        b2 = jnp.zeros((E, H), dtype=jnp.float32)
        return {'x': x, 'gate_w': gate_w, 'w1': w1, 'b1': b1, 'w2': w2, 'b2': b2}
    _L0_ffn_all = _L0_ffn_setup()
    _L0_ffn_in = {k: v for k, v in _L0_ffn_all.items() if k in ('gate_w', 'w1', 'b1', 'w2', 'b2')}
    del _L0_ffn_all
    return {'x': x, 'ctx_1024': ctx_1024, 'mask_Bx1x1xS2_fk0': mask_Bx1x1xS2_fk0, 'L0_attn_Wq': _L0_attn_in['Wq'], 'L0_attn_bq': _L0_attn_in['bq'], 'L0_attn_Wk': _L0_attn_in['Wk'], 'L0_attn_bk': _L0_attn_in['bk'], 'L0_attn_Wv': _L0_attn_in['Wv'], 'L0_attn_bv': _L0_attn_in['bv'], 'L0_attn_Wo': _L0_attn_in['Wo'], 'L0_attn_bo': _L0_attn_in['bo'], 'L0_xattn_Wq': _L0_xattn_in['Wq'], 'L0_xattn_bq': _L0_xattn_in['bq'], 'L0_xattn_Wk': _L0_xattn_in['Wk'], 'L0_xattn_bk': _L0_xattn_in['bk'], 'L0_xattn_Wv': _L0_xattn_in['Wv'], 'L0_xattn_bv': _L0_xattn_in['bv'], 'L0_xattn_Wo': _L0_xattn_in['Wo'], 'L0_xattn_bo': _L0_xattn_in['bo'], 'L0_ffn_gate_w': _L0_ffn_in['gate_w'], 'L0_ffn_w1': _L0_ffn_in['w1'], 'L0_ffn_b1': _L0_ffn_in['b1'], 'L0_ffn_w2': _L0_ffn_in['w2'], 'L0_ffn_b2': _L0_ffn_in['b2']}

def reference(x, ctx_1024, mask_Bx1x1xS2_fk0, L0_attn_Wq, L0_attn_bq, L0_attn_Wk, L0_attn_bk, L0_attn_Wv, L0_attn_bv, L0_attn_Wo, L0_attn_bo, L0_xattn_Wq, L0_xattn_bq, L0_xattn_Wk, L0_xattn_bk, L0_xattn_Wv, L0_xattn_bv, L0_xattn_Wo, L0_xattn_bo, L0_ffn_gate_w, L0_ffn_w1, L0_ffn_b1, L0_ffn_w2, L0_ffn_b2):
    import jax
    import jax.numpy as jnp

    def _L0_attn_ref(x, Wq, bq, Wk, bk, Wv, bv, Wo, bo):
        import jax, jax.numpy as jnp
        import numpy as np
        import math
        NUM_HEADS = 16

        def _alibi_bias(L, num_heads):
            slopes = jnp.power(2.0, jnp.linspace(-4.0, -0.3, num_heads))
            pos = jnp.arange(L, dtype=jnp.float32)
            return -(slopes[:, None] * pos[None, :])
        B, L, D = x.shape
        H = NUM_HEADS
        hd = D // H
        scale = math.sqrt(hd)

        def proj(W, b):
            return (jnp.einsum('bld,ed->ble', x, W) + b).reshape(B, L, H, hd)
        q = proj(Wq, bq)
        k = proj(Wk, bk)
        v = proj(Wv, bv)
        scores = jnp.einsum('bqhd,bkhd->bhqk', q, k) / scale
        bias = _alibi_bias(L, H)
        scores = scores + bias[None, :, None, :]
        attn = jax.nn.softmax(scores, axis=-1)
        out = jnp.einsum('bhqk,bkhd->bqhd', attn, v).reshape(B, L, D)
        return jnp.einsum('bld,ed->ble', out, Wo) + bo

    def _L0_xattn_ref(v, k, q, mask, Wq, bq, Wk, bk, Wv, bv, Wo, bo):
        import jax, jax.numpy as jnp
        import numpy as np
        B, S, D, H = (4, 512, 256, 16)
        DEPTH = D // H

        def _split_heads(x):
            b, s, _ = x.shape
            return x.reshape(b, s, H, DEPTH).transpose(0, 2, 1, 3)
        qh = _split_heads(q @ Wq + bq)
        kh = _split_heads(k @ Wk + bk)
        vh = _split_heads(v @ Wv + bv)
        logits = jnp.einsum('bhqd,bhkd->bhqk', qh, kh) / jnp.sqrt(jnp.asarray(DEPTH, dtype=qh.dtype))
        logits = logits + mask * -1000000000.0
        attn = jax.nn.softmax(logits, axis=-1)
        out = jnp.einsum('bhqk,bhkd->bhqd', attn, vh)
        out = out.transpose(0, 2, 1, 3).reshape(q.shape[0], -1, D)
        return out @ Wo + bo

    def _L0_ffn_ref(x, gate_w, w1, b1, w2, b2):
        import jax, jax.numpy as jnp
        import numpy as np
        TEMPERATURE = 1.0
        TOPK = 2
        s, b, h = x.shape
        x_flat = x.reshape(s * b, h)
        logits = x_flat @ gate_w.T
        probs = jax.nn.softmax(logits / TEMPERATURE, axis=-1)
        topk_probs, topk_idx = jax.lax.top_k(probs, TOPK)
        hidden = jax.nn.relu(jnp.einsum('th,ehf->tef', x_flat, w1) + b1[None])
        all_out = jnp.einsum('tef,efh->teh', hidden, w2) + b2[None]
        gathered = jnp.take_along_axis(all_out, topk_idx[:, :, None], axis=1)
        y_flat = jnp.sum(gathered * topk_probs[:, :, None], axis=1)
        return y_flat.reshape(s, b, h)
    x = _layernorm(x + _L0_attn_ref(x, L0_attn_Wq, L0_attn_bq, L0_attn_Wk, L0_attn_bk, L0_attn_Wv, L0_attn_bv, L0_attn_Wo, L0_attn_bo), axis=-1)
    x = _layernorm(x + _L0_xattn_ref(ctx_1024, ctx_1024, x, mask_Bx1x1xS2_fk0, L0_xattn_Wq, L0_xattn_bq, L0_xattn_Wk, L0_xattn_bk, L0_xattn_Wv, L0_xattn_bv, L0_xattn_Wo, L0_xattn_bo), axis=-1)
    x = _layernorm(x + _L0_ffn_ref(x, L0_ffn_gate_w, L0_ffn_w1, L0_ffn_b1, L0_ffn_w2, L0_ffn_b2), axis=-1)
    return x

_drawn_inputs = setup_inputs


def setup_inputs(seed=0):
    import zlib

    import numpy as np

    out = dict(_drawn_inputs(seed))
    spreads = {'L0_xattn_bq': (0.0, 0.1),
     'L0_xattn_bk': (0.0, 2.0),
     'L0_xattn_bv': (0.0, 0.1),
     'L0_xattn_bo': (0.0, 0.1),
     'L0_ffn_b1': (0.0, 0.1),
     'L0_ffn_b2': (0.0, 0.1)}
    factors = {'L0_attn_Wq': 5.654,
     'L0_attn_bq': 26.102,
     'L0_attn_Wk': 6.416,
     'L0_attn_bk': 64.0,
     'L0_attn_bv': 3.293}
    for name, (base, spread) in spreads.items():
        noise = np.random.default_rng([zlib.crc32(name.encode()), seed]).standard_normal(out[name].shape)
        drawn = base * np.exp(spread * noise) if base else spread * noise
        out[name] = jnp.asarray(drawn.astype(out[name].dtype))
    for name, factor in factors.items():
        out[name] = (out[name] * factor).astype(out[name].dtype)
    return out
```

```python
from contextlib import ExitStack

import numpy as np

import concourse.bass as bass
from concourse import mybir

ALU = mybir.AluOpType
ACT = mybir.ActivationFunctionType
AX = mybir.AxisListType
F32 = mybir.dt.float32
BF16 = mybir.dt.bfloat16
F16 = mybir.dt.float16
I32 = mybir.dt.int32
U32 = mybir.dt.uint32

P = 128
B, L, D = 16, 256, 256
LC = 120
H, HD = 16, 16
NE, F = 8, 1024
T = B * L
KT = D // P
QT = L // P
HM = H // KT
NG = 4
GH = H // NG
PROD = 96
AUX = 15
PARTS = 3
NT = T // P
NBLK = 2 * T // P + NE - 1
ROW = D + 4
FT = F // P
WC = KT * F
SQ = 1.0 / float(np.sqrt(HD))
EPS = 1e-5
Q_RUNS = [(0, 0, 3), (3, 0, 2), (5, 0, 1)]
K_BLOCKS = [0, 0, 0, 1, 1, 2]


class Chain:

    def __init__(self, eng, sem, nc=None, held=None):
        self.nc, self.eng, self.sem, self.held, self.n, self.count = nc, eng, sem, held, 0, 0

    def __call__(self, ins):
        ins.then_inc(self.sem, 1)
        self.n = self.n + 1
        self.count += 1
        if self.held:
            apart(self.nc, self.eng, self.sem, self.n, self.held)
        else:
            self.eng.wait_ge(self.sem, self.n)


def apart(nc, eng, sem, value, held):
    value = value if isinstance(value, int) else nc.snap(value)
    eng.wait_ge(*held)
    eng.wait_ge(sem, value)


def emit(nc, ap):
    ctx = ExitStack()
    with ctx:
        build(nc, ctx, ap)


def build(nc, ctx, ap):
    def sb(name, shape, dt=F32):
        return ctx.enter_context(nc.sbuf_tensor(name, shape, dt))

    sems = {}

    def sem(name):
        if name not in sems:
            sems[name] = ctx.enter_context(nc.semaphore(name))
        return sems[name]

    ident = sb("ident", [P, P])
    identb = sb("identb", [P, P], BF16)
    mhalf = sb("mhalf", [P, 4])
    LG = sb("LG", [P, NT, NE])
    X2R = sb("X2R", [P, NT, ROW])
    SC = sb("SC", [P, 5])
    b1c = sb("b1c", [P, NE, FT])
    dW = nc.dram_tensor("d_w", [NE, P, 2, 2, WC], F16).ap()
    XS = nc.dram_tensor("d_rows", [NBLK * P, ROW], F32).ap()
    YS = nc.dram_tensor("d_sums", [T + P, D], F32).ap()
    outer = dict(ident=ident, identb=identb, mhalf=mhalf, LG=LG, X2R=X2R, SC=SC, b1c=b1c, dW=dW, XS=XS, YS=YS)
    with ExitStack() as inner:
        attention(nc, inner, ap, outer, sem)
    with ExitStack() as inner:
        experts(nc, inner, ap, outer, sem)


def attention(nc, ctx, ap, outer, sem):
    ident, identb, mhalf, LG, X2R, SC, b1c, dW, XS, YS = (outer[n] for n in (
        "ident", "identb", "mhalf", "LG", "X2R", "SC", "b1c", "dW", "XS", "YS"))

    def sb(name, shape, dt=F32):
        return ctx.enter_context(nc.sbuf_tensor(name, shape, dt))

    def ps(name, shape, dt=F32):
        return ctx.enter_context(nc.psum_tensor(name, shape, dt))

    wq, wk, wv, wo = (sb(n, [P, KT, D]) for n in ("wq", "wk", "wv", "wo"))
    cq, ck, cv, co = (sb(n, [P, KT, D]) for n in ("cq", "ck", "cv", "co"))
    cols = sb("cols", [P, 4, KT])
    rows_b = sb("rows_b", [P, 4, D])
    maskt = sb("maskt", [B, LC])
    maskr = sb("maskr", [B, 2, LC])
    maskp = sb("maskp", [B, PARTS, LC], BF16)

    xT = sb("xT", [P, KT, L])
    cT = sb("cT", [P, KT, LC])
    xrow = sb("xrow", [P, QT, D])
    xbo = sb("xbo", [P, QT, D])
    x1T = sb("x1T", [P, KT, L])
    names = ("q", "k", "cq", "ck")
    width = dict(q=L, k=L, cq=L, ck=LC)
    full = {n: sb(f"{n}_full", [P, KT, width[n]]) for n in names}
    rest = {n: sb(f"{n}_rest", [P, KT, width[n]]) for n in names}
    part = {n: sb(f"{n}_part", [P, KT, PARTS, width[n]], BF16) for n in names}
    stack = {n: sb(f"{n}_stack", [PROD + AUX, H, width[n]], BF16) for n in names}
    V = sb("V", [P, QT, H, 2 * HD])
    CV = sb("CV", [P, H, 2 * HD])
    PT = sb("PT", [P, 2, GH, 2, L])
    mneg = sb("mneg", [P, QT, GH])
    mr = sb("mr", [P, QT, GH])
    MTp = sb("MTp", [P, QT, 16], BF16)
    mts = sb("mts", [16, L], BF16)
    avs = sb("avs", [P, L])
    rc = sb("rc", [P, QT, GH])
    ao = sb("ao", [P, QT, D])
    aoT = sb("aoT", [P, KT, L])
    r1 = sb("r1", [P, QT, D])
    stats = sb("stats", [P, QT, 6])
    mv = sb("mv", [P, QT, 2])
    ve = sb("ve", [P, QT])
    rstd = sb("rstd", [P, QT])
    x1s = sb("x1s", [P, QT, D])
    x1bo = sb("x1bo", [P, QT, D])
    x2s = sb("x2s", [P, QT, D])
    x2T = sb("x2T", [P, KT, L])
    gate = sb("gate", [P, KT, NE])
    wst = [sb(f"wst{k}", [P, WC]) for k in range(2)]
    w16 = [sb(f"w16_{k}", [P, 2, WC], F16) for k in range(2)]
    wmx = sb("wmx", [P, 2, NG, NE])
    wm = sb("wm", [P, 3])
    wg = sb("wg", [P, 3])
    wp = sb("wp", [P, 8])
    b1t = sb("b1t", [P, NE, FT])
    fill = sb("fill", [P, ROW])

    SA = ps("SA", [P, 2, 512])
    SB = ps("SB", [P, 2, 512])
    AV = ps("AV", [P, 512])
    MT = ps("MT", [16, 1024], BF16)
    BK = [ps("BK0", [P, 512]), ps("BK1", [P, 512])]

    dpart = {n: nc.dram_tensor(f"d_{n}", [KT, PARTS, P, width[n]], BF16).ap() for n in names}
    dmask = nc.dram_tensor("d_mask", [B, PARTS, LC], BF16).ap()

    def on(b):
        return not isinstance(b, int) or 0 <= b < B

    def wait(eng, name, val):
        if not isinstance(val, int) or val > 0:
            eng.wait_ge(sem(name), val)

    def wait_apart(eng, name, val, held, count):
        if not isinstance(val, int) or val > 0:
            apart(nc, eng, sem(name), val, (sem(held), count))

    ITEMS = [[("Q", 1), ("T1", -1), ("AOTc", -2), ("Kc", 0), ("T2", -2), ("AOT", 0)],
             [("Qc", -1), ("Vc", -1), ("Oc", -2), ("K", 1), ("V", 1), ("O", 0), ("R", -2)]]
    BANK = {n: k for k in range(2) for n, _ in ITEMS[k]}

    def bank_free(eng, name, i):
        order = ITEMS[BANK[name]]
        at = [n for n, _ in order].index(name)
        for back in range(1, 14):
            pos = at - back
            n, off = order[pos % len(order)]
            b = i + off + pos // len(order)
            if on(b):
                wait(eng, f"read_{n}", b + 1)
                return

    def iterations(step, eng, chain=None, per=0):
        for i in (-1, 0, 1, 2):
            step(i, "max")
        looped(step, eng, 3, 6, "max", chain, per)
        step(6, "max")
        step(7, "scale")
        step(8, "halve")
        looped(step, eng, 9, B - 2, "halve", chain, per)
        step(B - 2, "halve")
        step(B - 1, "halve")
        step(B, None)
        step(B + 1, None)

    def looped(step, eng, first, end, mode, chain, per):
        n = chain.n if chain else 0
        with eng.Fori(first, end) as i:
            if chain:
                chain.n, chain.count = n + per * (i - first), 0
            step(i, mode)
            assert not chain or chain.count == per, chain.count
        if chain:
            chain.n = n + per * (end - first)

    def group(u, i, back):
        n = u - back
        if n < 0:
            n, i = n + 2 * NG, i - 1
        return (True, i, n) if n < NG else (False, i - 1, n - NG)

    def last(eng, u, i, back, what, per=1):
        for more in range(8):
            if u - back - more < -8:
                return
            mine, b, g = group(u, i, back + more)
            if on(b):
                n = per if mine else 1
                wait(eng, what + ("" if mine else "c"), n * (NG * b + g + 1))
                return

    GAPS = {(0, 0): ("Q", 1), (0, 1): ("T1", -1), (1, 0): ("Qc", -1), (2, 0): ("Vc", -1),
            (2, 1): ("AOTc", -2), (3, 0): ("Oc", -2), (4, 0): ("K", 1), (4, 1): ("Kc", 0),
            (5, 0): ("T2", -2), (5, 1): ("V", 1), (6, 1): ("AOT", 0), (7, 0): ("O", 0), (7, 1): ("R", -2)}

    block = ctx.enter_context(nc.Block())

    N_Q, N_K = len(Q_RUNS), len(K_BLOCKS)
    QW = WC // NG

    @block.sync
    def _(sp):
        for dst, src in ((wq, "wq"), (wk, "wk"), (wv, "wv")):
            sp.dma_start(dst[:, :, :], ap[src].rearrange("(k p) n -> p k n", p=P)).then_inc(sem("ld_w"), 16)
        sp.dma_start(xT[:, :, :], ap["xT"][0].rearrange("(k p) n -> p k n", p=P)).then_inc(sem("ld_xT"), 16)
        for n, name in enumerate(("bq", "bk", "cbq", "cbk")):
            sp.dma_start(cols[:, n, :], ap[name]).then_inc(sem("ld_cols"), 16)
        for n, name in enumerate(("bv", "bo", "cbv", "cbo")):
            sp.dma_start(rows_b[:, n, :], ap[name].partition_broadcast(P)).then_inc(sem("ld_rows"), 16)
        sp.dma_start(cT[:, :, :], ap["ctxT"][0].rearrange("(k p) n -> p k n", p=P)).then_inc(sem("ld_cT"), 16)
        sp.dma_start(maskt[:, :], ap["mask"]).then_inc(sem("ld_mask"), 16)
        sp.dma_start(ident[:, :], ap["ident"]).then_inc(sem("ld_const"), 16)
        sp.dma_start(gate[:, :, :], ap["gate"].rearrange("(k p) n -> p k n", p=P)).then_inc(sem("ld_gate"), 16)
        auxf = PT[PROD:PROD + AUX, :, :, :, :].rearrange("p a h k n -> p (a h k n)")
        for n, name in enumerate(names):
            if n >= 1:
                sp.wait_ge(sem("aux_set"), n)
            sp.dma_start(auxf[:, 0:H * width[name]],
                         ap[f"aux_{name}"].rearrange("p h n -> p (h n)")).then_inc(sem("ld_aux"), 16)
        for dst, src in ((wo, "wo"), (cq, "cwq"), (ck, "cwk"), (cv, "cwv"), (co, "cwo")):
            sp.dma_start(dst[:, :, :], ap[src].rearrange("(k p) n -> p k n", p=P)).then_inc(sem("ld_w2"), 16)
        sp.dma_start(fill[:, :], ap["fill"]).then_inc(sem("ld_fill"), 16)
        sp.dma_start(b1t[:, :, :], ap["b1t"]).then_inc(sem("ld_b1"), 16)
        sp.wait_ge(sem("ld_fill"), 16)
        sp.dma_start(XS.rearrange("(j p) c -> p j c", p=P),
                     fill[:, :].unsqueeze(1).to_broadcast([P, NBLK, ROW])).then_inc(sem("wr_fill"), 16)
        sp.dma_start(YS[T:T + P, :], fill[:, 0:D]).then_inc(sem("wr_fill"), 16)
        sp.wait_ge(sem("mask_parts"), 1)
        sp.dma_start(dmask, maskp[:, :, :]).then_inc(sem("wr_mask"), 16)
        sp.wait_ge(sem("wr_mask"), 16)

        def write_parts(n, b):
            wait(sp, f"parts_{n}", b + 1)
            sp.dma_start(dpart[n].rearrange("k a p t -> p (k a) t"),
                         part[n][:, :, :, :].rearrange("p k a t -> p (k a) t")).then_inc(sem(f"wr_{n}"), 16)

        def read_stack(n, b, blocks):
            wait(sp, f"wr_{n}", (b + 1) * 16)
            for block0, part0, count in blocks:
                src = dpart[n].rearrange("k a (d m) t -> k (a d) (m t)", m=HM)
                src = src[:, part0 * HD:(part0 + count) * HD, :].rearrange("k p n -> p k n")
                dst = stack[n][block0 * HD:(block0 + count) * HD, :, :].rearrange(
                    "p (k m) t -> p k (m t)", k=KT)
                sp.dma_start(dst, src).then_inc(sem(f"st_{n}"), 16)

        k_runs = [(n, a, 1) for n, a in enumerate(K_BLOCKS)]

        def load_expert(e, k):
            src = (ap["w1"] if k == 0 else ap["w2"])[bass.ds(e, 1)]
            sp.dma_start(wst[k][:, :].rearrange("p (a n) -> p a n", a=KT if k == 0 else FT),
                         src.rearrange("e (a p) n -> p (e a) n", p=P)).then_inc(sem(f"ld_wst{k}"), 16)

        def experts_in(i, mode, k):
            if mode == "max":
                wait(sp, f"wmax{k}", i + 1)
                load_expert(i + 1, k)
            elif mode == "halve":
                load_expert(i - 8, k)

        def experts_out(i, mode, k):
            if mode == "halve":
                wait(sp, f"wlo{k}", i - 7)
                sp.dma_start(dW[bass.ds(i - 8, 1), :, k].rearrange("e p a n -> p (e a) n"),
                             w16[k][:, :, :]).then_inc(sem(f"wr_w{k}"), 16)

        def step(i, mode):
            experts_in(i, mode, 1)
            if on(i):
                wait(sp, "xbo", i)
                sp.dma_start(xrow[:, :, :], ap["x"][bass.ds(i, 1)].rearrange("b (t p) d -> p (b t) d", p=P)
                             ).then_inc(sem("ld_x"), 16)
            if on(i - 1):
                wait_apart(sp, "STc", NG * (i - 1), "wr_mask", 16)
                read_stack("ck", i - 1, k_runs)
                sp.dma_start(stack["ck"][PROD:PROD + PARTS, :, :],
                             dmask[bass.ds(i - 1, 1)].rearrange("b a t -> (b a) t").unsqueeze(1)
                             .to_broadcast([PARTS, H, LC])).then_inc(sem("st_ck"), 16)
                write_parts("cq", i - 1)
                read_stack("cq", i - 1, Q_RUNS)
            if on(i + 1):
                write_parts("q", i + 1)
            if on(i) and not (isinstance(i, int) and i == 0):
                wait(sp, "Vc", i)
                sp.dma_start(cT[:, :, :], ap["ctxT"][bass.ds(i, 1)].rearrange("b (k p) n -> p (b k) n", p=P)
                             ).then_inc(sem("ld_cT"), 16)
            if on(i - 2):
                wait(sp, "x2", i - 1)
                sp.dma_start(YS[0:T, :].rearrange("(b t p) d -> b t p d", t=QT, p=P)[bass.ds(i - 2, 1)]
                             .rearrange("b t p d -> p (b t) d"), x2s[:, :, :]).then_inc(sem("wr_x2"), 16)
                sp.dma_start(X2R[:, bass.ds(QT * (i - 2), QT), 0:D], x2s[:, :, :]).then_inc(sem("wr_x2"), 16)
            experts_out(i, mode, 0)
            if mode == "scale":
                wait(sp, "wmax0", NE)
                experts_in(i + 1, "halve", 0)
            elif not (isinstance(i, int) and i in (6, B - 1)):
                experts_in(i + 1, mode, 0)
            if on(i + 1):
                write_parts("k", i + 1)
                wait_apart(sp, "ST", 2 * NG * (i + 1), "wr_mask", 16)
                read_stack("q", i + 1, Q_RUNS)
                read_stack("k", i + 1, k_runs)
            if on(i):
                write_parts("ck", i)
            if on(i + 2):
                wait(sp, "V", i + 2)
                sp.dma_start(xT[:, :, :], ap["xT"][bass.ds(i + 2, 1)].rearrange("b (k p) n -> p (b k) n", p=P)
                             ).then_inc(sem("ld_xT"), 16)
            experts_out(i, mode, 1)

        load_expert(0, 0)
        iterations(step, sp)

        sp.wait_ge(sem("wr_x2"), 32 * B)
        sp.wait_ge(sem("wr_fill"), 32)
        for k in range(2):
            sp.wait_ge(sem(f"wr_w{k}"), 16 * NE)

    @block.tensor
    def _(pe):
        pe.wait_ge(sem("ld_w"), 48)

        def put_cols(name, w, rhs, n):
            out = BK[BANK[name]][:, :].rearrange("p (k n) -> p k n", k=KT)
            for m in range(KT):
                for k in range(KT):
                    mm = pe.matmul(out[:, m, 0:n], w[:, k, m * P:(m + 1) * P], rhs[:, k, :],
                                   start=(k == 0), stop=(k == KT - 1))
            mm.then_inc(sem(name), 1)

        def put_rows(name, lhs, w, tiles, m):
            out = BK[BANK[name]][:, :].rearrange("p (t n) -> p t n", n=D)
            for t in range(tiles):
                for k in range(KT):
                    mm = pe.matmul(out[0:m, t, :], lhs[:, k, t * P:t * P + m], w[:, k, :],
                                   start=(k == 0), stop=(k == KT - 1))
            mm.then_inc(sem(name), 1)

        def put_turned(name, src):
            out = BK[BANK[name]][:, :].rearrange("p (k n) -> p k n", k=KT)
            for k in range(KT):
                for t in range(QT):
                    mm = pe.transpose(out[:, k, t * P:(t + 1) * P], src[:, t, k * P:(k + 1) * P], ident[:, :])
            mm.then_inc(sem(name), 1)

        def item(name, b, i):
            if not on(b):
                return
            bank_free(pe, name, i)
            if name == "Q":
                wait(pe, "ld_xT", 16 * (b + 1))
                put_cols(name, wq, xT, L)
            elif name == "K":
                put_cols(name, wk, xT, L)
            elif name == "V":
                put_rows(name, xT, wv, QT, P)
            elif name == "T1":
                if isinstance(i, int) and i <= 1:
                    wait(pe, "ld_const", 16)
                    wait(pe, "ld_w2", 80)
                wait(pe, "x1", b + 1)
                put_turned(name, x1s)
            elif name == "Qc":
                wait(pe, "read_T1", b + 1)
                put_cols(name, cq, x1T, L)
            elif name == "Kc":
                if isinstance(i, int) and i == 0:
                    wait(pe, "ld_w2", 80)
                wait(pe, "ld_cT", 16 * (b + 1))
                put_cols(name, ck, cT, LC)
            elif name == "Vc":
                put_rows(name, cT, cv, 1, LC)
            elif name in ("AOT", "AOTc"):
                wait(pe, "norm" if name == "AOT" else "normc", NG * (b + 1))
                if isinstance(i, int) and i <= 0:
                    wait(pe, "ld_const", 16)
                put_turned(name, ao)
            elif name in ("O", "Oc"):
                wait(pe, "read_AOT" if name == "O" else "read_AOTc", b + 1)
                put_rows(name, aoT, wo if name == "O" else co, QT, P)
            elif name == "T2":
                wait(pe, "x2", b + 1)
                put_turned(name, x2s)
            elif name == "R":
                if isinstance(i, int):
                    wait(pe, "ld_gate", 16)
                wait(pe, "read_T2", b + 1)
                for t in range(QT):
                    for k in range(KT):
                        mm = pe.matmul(BK[1][:, t * NE:(t + 1) * NE], x2T[:, k, t * P:(t + 1) * P],
                                       gate[:, k, :], start=(k == 0), stop=(k == KT - 1))
                mm.then_inc(sem(name), 1)

        def scores(u, half, i):
            if u < NG:
                b, g = i, u
                if not on(b):
                    return
                wait(pe, "max", 2 * NG * b + 2 * g + half)
                if g == 0 and half == 0:
                    wait(pe, "maxc", NG * (i - 1))
                    if isinstance(i, int) and i == 0:
                        wait(pe, "aux_set", 4)
                    wait(pe, "st_q", 16 * N_Q * (b + 1))
                    wait(pe, "st_k", 16 * N_K * (b + 1))
                for j in range(2):
                    h = GH * g + 2 * half + j
                    for t in range(QT):
                        mm = pe.matmul(SA[:, j, t * L:(t + 1) * L],
                                       stack["q"][0:PROD + PARTS, h, t * P:(t + 1) * P],
                                       stack["k"][0:PROD + PARTS, h, :], start=True, stop=True)
                mm.then_inc(sem("S"), 1)
            elif half == 0:
                b, g = i - 1, u - NG
                if not on(b):
                    return
                wait(pe, "maxc", NG * b + g)
                if g == 0:
                    wait(pe, "max", 2 * NG * (i + 1) if on(i) else 2 * NG * B)
                    wait(pe, "st_cq", 16 * N_Q * (b + 1))
                    wait(pe, "st_ck", 16 * (N_K + 1) * (b + 1))
                for j in range(GH):
                    h = GH * g + j
                    for t in range(QT):
                        at = (2 * (j % 2) + t) * LC
                        mm = pe.matmul(SA[:, j // 2, at:at + LC],
                                       stack["cq"][0:PROD + PARTS, h, t * P:(t + 1) * P],
                                       stack["ck"][0:PROD + PARTS, h, :], start=True, stop=True)
                mm.then_inc(sem("Sc"), 1)

        def maxima(u, i):
            mine, b, g = group(u, i, 1)
            if not on(b):
                return
            c = "" if mine else "c"
            wait(pe, f"mparts{c}", NG * b + g + 1)
            last(pe, u, i, 2, "mcopy")
            for t in range(QT):
                mm = pe.transpose(MT[0:AUX, t * P:(t + 1) * P], MTp[:, t, 0:AUX], identb[:, :])
            mm.then_inc(sem(f"MT{c}"), 1)

        def keyed(u, half, i):
            mine, b, g = group(u, i, 1)
            if not on(b) or (not mine and half == 1):
                return
            if half == 0:
                last(pe, u, i, 2, "E", 2)
            if mine:
                if half == 0:
                    wait(pe, "aux", NG * b + g + 1)
                else:
                    wait(pe, "E", 2 * (NG * b + g) + 1)
                for j in range(2):
                    h = GH * g + 2 * half + j
                    for k in range(QT):
                        mm = pe.matmul(SB[:, j, k * L:(k + 1) * L],
                                       stack["k"][:, h, k * P:(k + 1) * P],
                                       stack["q"][:, h, :], start=True, stop=True)
                mm.then_inc(sem("ST"), 1)
            else:
                wait(pe, "auxc", NG * b + g + 1)
                for j in range(GH):
                    h = GH * g + j
                    mm = pe.matmul(SB[0:LC, j // 2, (j % 2) * L:(j % 2 + 1) * L],
                                   stack["ck"][:, h, :], stack["cq"][:, h, :], start=True, stop=True)
                mm.then_inc(sem("STc"), 1)

        def weigh(u, i):
            mine, b, g = group(u, i, 2)
            if not on(b):
                return
            c = "" if mine else "c"
            last(pe, u, i, 3, "norm")
            wait(pe, f"E{c}", (2 if mine else 1) * (NG * b + g + 1))
            wait(pe, f"read_V{c}", b + 1)
            slot = u % 2
            for k in range(QT if mine else 1):
                for j in range(GH):
                    h = GH * g + j
                    if mine:
                        mm = pe.matmul(AV[32 * j:32 * j + 32, 0:L], V[:, k, h, :], PT[:, slot, j, k, :],
                                       start=(k == 0), stop=(k == QT - 1))
                    else:
                        mm = pe.matmul(AV[32 * j:32 * j + 32, 0:L], CV[0:LC, h, :],
                                       PT[0:LC, slot, j, 0, :], start=True, stop=True)
            mm.then_inc(sem(f"AV{c}"), 1)

        def turn_weighed(u, i):
            mine, b, g = group(u, i, 3)
            if not on(b):
                return
            c = "" if mine else "c"
            wait(pe, f"avs{c}", NG * b + g + 1)
            for t in range(QT):
                mm = pe.transpose(AV[:, t * P:(t + 1) * P], avs[:, t * P:(t + 1) * P], ident[:, :])
            mm.then_inc(sem(f"AVT{c}"), 1)

        def gap(u, half, i):
            if (u, half) in GAPS:
                name, off = GAPS[u, half]
                item(name, i + off, i)

        def step(i, mode):
            for u in range(2 * NG):
                maxima(u, i)
                scores(u, 0, i)
                turn_weighed(u, i)
                gap(u, 0, i)
                scores(u, 1, i)
                keyed(u, 0, i)
                weigh(u, i)
                keyed(u, 1, i)
                gap(u, 1, i)

        iterations(step, pe)

    @block.vector
    def _(dve):
        chain = Chain(dve, sem("dve_chain"))

        auxf = PT[PROD:PROD + AUX, :, :, :, :].rearrange("p a h k n -> p (a h k n)")
        for n, name in enumerate(names):
            dve.wait_ge(sem("ld_aux"), 16 * (n + 1))
            dve.tensor_copy(stack[name][PROD:PROD + AUX, :, :].rearrange("p h n -> p (h n)"),
                            auxf[:, 0:H * width[name]]).then_inc(sem("aux_set"), 1)
        dve.memset(MTp[:, :, :], 1.0)
        dve.wait_ge(sem("ld_const"), 16)
        dve.tensor_copy(identb[:, :], ident[:, :]).then_inc(sem("identb"), 1)
        dve.wait_ge(sem("ld_cols"), 64)
        for n in (1, 3):
            dve.tensor_scalar(cols[:, n, :], cols[:, n, :], SQ, None, ALU.mult).then_inc(sem("cols"), 1)
        dve.wait_ge(sem("ld_mask"), 16)
        chain(dve.tensor_scalar(maskr[:, 0, :], maskt[:, :], -1e9, None, ALU.mult))
        chain(dve.tensor_copy(maskp[:, 0, :], maskr[:, 0, :]))
        chain(dve.tensor_tensor(maskr[:, 1, :], maskr[:, 0, :], maskp[:, 0, :], ALU.subtract))
        chain(dve.tensor_copy(maskp[:, 1, :], maskr[:, 1, :]))
        dve.tensor_tensor(maskp[:, 2, :], maskr[:, 1, :], maskp[:, 1, :], ALU.subtract).then_inc(sem("mask_parts"), 1)

        def top(u, half, i):
            mine, b, g = group(u, i, 0)
            if not on(b) or (not mine and half == 1):
                return
            if mine:
                wait(dve, "S", 2 * (NG * b + g) + half + 1)
                dve.tensor_reduce(mneg[:, :, 2 * half:2 * half + 2].rearrange("p t j -> p j t"),
                                  SA[:, :, :].rearrange("p j (t n) -> p j t n", n=L),
                                  AX.X, ALU.max, negate=True).then_inc(sem("max"), 1)
            else:
                wait(dve, "Sc", NG * b + g + 1)
                dve.tensor_reduce(mneg[:, :, :].rearrange("p t j -> p j t"),
                                  SA[:, :, 0:4 * LC].rearrange("p a (c n) -> p a c n", n=LC),
                                  AX.X, ALU.max, negate=True).then_inc(sem("maxc"), 1)

        def spread_maxima(u, i):
            mine, b, g = group(u, i, 1)
            if not on(b):
                return
            c, q = ("", "q") if mine else ("c", "cq")
            wait(dve, f"MT{c}", NG * b + g + 1)
            dve.tensor_copy(mts[0:AUX, :], MT[0:AUX, 0:L]).then_inc(sem(f"mcopy{c}"), 1)
            wait(dve, f"mcopy{c}", NG * b + g + 1)
            dve.tensor_copy(stack[q][PROD:PROD + AUX, GH * g:GH * g + GH, :],
                            mts[0:AUX, :].unsqueeze(1).to_broadcast([AUX, GH, L])
                            ).then_inc(sem(f"aux{c}"), 1)

        def split_maxima(u, i):
            mine, b, g = group(u, i, 0)
            if not on(b):
                return
            c = "" if mine else "c"
            wait(dve, f"max{c}", (2 if mine else 1) * (NG * b + g + 1))
            p0, p1, p2 = (MTp[:, :, 3 + GH * a:3 + GH * (a + 1)] for a in range(PARTS))
            chain(dve.tensor_copy(p0, mneg[:, :, :]))
            chain(dve.tensor_tensor(mr[:, :, :], mneg[:, :, :], p0, ALU.subtract))
            chain(dve.tensor_copy(p1, mr[:, :, :]))
            dve.tensor_tensor(p2, mr[:, :, :], p1, ALU.subtract).then_inc(sem(f"mparts{c}"), 1)

        def divide(u, i):
            mine, b, g = group(u, i, 3)
            if not on(b):
                return
            c = "" if mine else "c"
            wait(dve, f"AVT{c}", NG * b + g + 1)
            turned = AV[:, 0:QT * P].rearrange("p (t j c) -> p t j c", t=QT, c=2 * HD)
            chain(dve.reciprocal(rc[:, :, :], turned[:, :, :, HD]))
            if g == 0:
                wait(dve, "AOT", i if mine else i + 1) if on(i) else wait(dve, "AOT", B)
                wait(dve, "AOTc", b - 1 if mine else b)
            dve.tensor_tensor(ao[:, :, GH * HD * g:GH * HD * (g + 1)].rearrange("p t (j c) -> p t j c", c=HD),
                              turned[:, :, :, 0:HD],
                              rc[:, :, :].unsqueeze(3).to_broadcast([P, QT, GH, HD]), ALU.mult
                              ).then_inc(sem(f"norm{c}"), 1)

        def item(name, b, i):
            if not on(b) or name not in ("V", "Vc", "O", "Oc", "R"):
                return
            wait(dve, name, b + 1)
            if name == "V":
                wait(dve, "ld_rows", 64) if isinstance(i, int) and i < 0 else None
                wait(dve, "ones", 3) if isinstance(i, int) and i < 0 else None
                wait(dve, "AV", NG * b)
                dve.tensor_tensor(V[:, :, :, 0:HD],
                                  BK[1][:, :].rearrange("p (t h d) -> p t h d", t=QT, d=HD),
                                  rows_b[:, 0, :].rearrange("p (h d) -> p h d", d=HD).unsqueeze(1)
                                  .to_broadcast([P, QT, H, HD]), ALU.add).then_inc(sem("read_V"), 1)
            elif name == "Vc":
                wait(dve, "AVc", NG * b)
                dve.tensor_tensor(CV[0:LC, :, 0:HD], BK[1][0:LC, 0:D].rearrange("p (h d) -> p h d", d=HD),
                                  rows_b[0:LC, 2, :].rearrange("p (h d) -> p h d", d=HD), ALU.add
                                  ).then_inc(sem("read_Vc"), 1)
            elif name == "R":
                dve.tensor_copy(LG[:, bass.ds(QT * b, QT), :].rearrange("p t n -> p (t n)"),
                                BK[1][:, 0:QT * NE]).then_inc(sem("read_R"), 1)
            else:
                c = name[1:]
                wait(dve, "xbo" if name == "O" else "x1bo", b + 1)
                dve.tensor_tensor(r1[:, :, :], BK[1][:, :].rearrange("p (t n) -> p t n", n=D),
                                  (xbo if name == "O" else x1bo)[:, :, :], ALU.add
                                  ).then_inc(sem(f"read_{name}"), 1)
                wait(dve, f"read_{name}", b + 1)
                for t in range(QT):
                    ins = dve.bn_stats(stats[:, t, :], r1[:, t, :])
                    ins.then_inc(sem(f"stats{c}"), 1)
                wait_apart(dve, f"stats{c}", QT * (b + 1), "identb", 1)
                for t in range(QT):
                    dve.bn_aggr(mv[:, t, :], stats[:, t, :]).then_inc(sem(f"mv{c}"), 1)

        def late(name, b, i):
            if not on(b):
                return
            c = name[1:]
            wait(dve, f"rstd{c}", b + 1)
            if c:
                wait(dve, "wr_x2", 32 * b)
            else:
                wait(dve, "x1bo", b)
            for t in range(QT):
                ins = dve.tensor_scalar((x2s if c else x1s)[:, t, :], r1[:, t, :], mv[:, t, 0:1],
                                        rstd[:, t:t + 1], ALU.subtract, ALU.mult)
            ins.then_inc(sem("x2" if c else "x1"), 1)

        def gap(u, half, i):
            if (u, half) in GAPS:
                name, off = GAPS[u, half]
                item(name, i + off, i)

        def weights(u, i, mode):
            if mode != "max":
                return
            k, c = divmod(u, NG)
            wait(dve, f"ld_wst{k}", 16 * (i + 2))
            ins = dve.tensor_reduce(wmx[:, k, c, bass.ds(i + 1, 1)], wst[k][:, c * QW:(c + 1) * QW], AX.X, ALU.max,
                                    apply_absolute_value=True)
            if c == NG - 1:
                ins.then_inc(sem(f"wmax{k}"), 1)

        def halves(u, i, mode):
            if mode != "halve":
                return
            k, c = divmod(u, NG)
            at = slice(c * QW, (c + 1) * QW)
            wait(dve, f"whi{k}", NG * (i - 8) + c + 1)
            ins = dve.scalar_tensor_tensor(w16[k][:, 1, at], wst[k][:, at], SC[:, k:k + 1], w16[k][:, 0, at],
                                           ALU.mult, ALU.subtract)
            if c == NG - 1:
                ins.then_inc(sem(f"wlo{k}"), 1)

        def greatest():
            dve.wait_ge(sem("ld_b1"), 16)
            for k in range(2):
                dve.wait_ge(sem(f"wmax{k}"), NE)
            dve.tensor_reduce(wm[:, 0:2], wmx[:, :, :, :].rearrange("p k c e -> p k (c e)"), AX.X, ALU.max)
            dve.tensor_reduce(wm[:, 2:3], b1t[:, :, :].rearrange("p e f -> p (e f)"), AX.X, ALU.max,
                              apply_absolute_value=True).then_inc(sem("wm"), 1)

        def scales():
            dve.wait_ge(sem("wg"), 1)
            chain(dve.tensor_copy(wp[:, 0:2], wg[:, 0:2]))
            chain(dve.tensor_scalar(wp[:, 2:3], wg[:, 0:1], float(D), wg[:, 2:3], ALU.mult, ALU.add))
            chain(dve.tensor_scalar(wp[:, 0:3], wp[:, 0:3], 2.0 ** -100, 2.0 ** 100, ALU.max, ALU.min))
            bits = wp[:, 0:3].bitcast(I32)
            chain(dve.tensor_scalar(bits, bits, 0x7F800000, None, ALU.bitwise_and))
            chain(dve.reciprocal(wp[:, 3:6], wp[:, 0:3]))
            chain(dve.tensor_scalar(SC[:, 0:2], wp[:, 3:5], 2.0 ** 13, None, ALU.mult))
            chain(dve.tensor_scalar(SC[:, 2:3], wp[:, 5:6], 2.0 ** 14, None, ALU.mult))
            chain(dve.tensor_scalar(SC[:, 3:4], SC[:, 2:3], wp[:, 0:1], 2.0 ** -13, ALU.mult, ALU.mult))
            chain(dve.tensor_scalar(SC[:, 4:5], wp[:, 1:2], wp[:, 2:3], 2.0 ** -27, ALU.mult, ALU.mult))
            dve.tensor_scalar(b1c[:, :, :], b1t[:, :, :], SC[:, 2:3], None, ALU.mult).then_inc(sem("scales"), 1)

        def step(i, mode):
            for u in range(2 * NG):
                if mode == "scale" and u == 0:
                    greatest()
                if mode == "scale" and u == 3:
                    scales()
                spread_maxima(u, i)
                top(u, 0, i)
                divide(u, i)
                if u == 4:
                    late("Oc", i - 2, i)
                if u == 0:
                    late("O", i - 1, i)
                top(u, 1, i)
                split_maxima(u, i)
                gap(u, 0, i)
                gap(u, 1, i)
                weights(u, i, mode)
                if u:
                    halves(u - 1, i, mode)
                if u == 2 * NG - 1:
                    halves(u, i, mode)

        iterations(step, dve, chain, 8 * 3 + 8)

    @block.scalar
    def _(act):
        def item(name, b, i):
            if not on(b) or name in ("V", "Vc", "O", "Oc", "R"):
                return
            wait(act, name, b + 1)
            bank = BK[BANK[name]][:, :].rearrange("p (k n) -> p k n", k=KT)
            if name in ("Q", "K", "Qc", "Kc"):
                n = dict(Q="q", K="k", Qc="cq", Kc="ck")[name]
                c = names.index(n)
                scale = SQ if name[0] == "K" else 1.0
                if isinstance(i, int) and i <= 1:
                    wait(act, "cols", 2)
                wait(act, f"parts_{n}", b)
                for k in range(KT):
                    ins = act.activation(full[n][:, k, :], bank[:, k, 0:width[n]], ACT.Identity,
                                         bias=cols[:, c, k:k + 1], scale=scale)
                    ins.then_inc(sem(f"read_{name}"), 1) if k == KT - 1 else ins.then_inc(sem(f"half_{name}"), 1)
                wait(act, f"read_{name}", b + 1)
                wait(act, f"half_{name}", b + 1)
                wait(act, f"wr_{n}", 16 * b)
                act.activation(part[n][:, :, 0, :], full[n][:, :, :], ACT.Copy).then_inc(sem(f"part0_{n}"), 1)
            else:
                dst = dict(T1=x1T, T2=x2T, AOT=aoT, AOTc=aoT)[name]
                act.activation(dst[:, :, :], bank, ACT.Copy).then_inc(sem(f"read_{name}"), 1)

        def gap(u, half, i):
            if (u, half) in GAPS:
                name, off = GAPS[u, half]
                item(name, i + off, i)

        def exps(u, half, i):
            mine, b, g = group(u, i, 1)
            if not on(b) or (not mine and half == 1):
                return
            slot = (u - 1) % 2
            if half == 0:
                last(act, u, i, 3, "AV")
                if isinstance(i, int) and i == 0:
                    wait(act, "aux_set", 4)
            if mine:
                wait(act, "ST", 2 * (NG * b + g) + half + 1)
                act.activation(PT[:, slot, 2 * half:2 * half + 2, :, :].rearrange("p j k n -> p (j k n)"),
                               SB[:, :, :].rearrange("p j n -> p (j n)"), ACT.Exp).then_inc(sem("E"), 1)
            else:
                wait(act, "STc", NG * b + g + 1)
                act.activation(PT[0:LC, slot, :, 0, :],
                               SB[0:LC, :, :].rearrange("p a (c n) -> p (a c) n", n=L), ACT.Exp
                               ).then_inc(sem("Ec"), 1)

        def store_weighed(u, i):
            mine, b, g = group(u, i, 2)
            if not on(b):
                return
            c = "" if mine else "c"
            wait(act, f"AV{c}", NG * b + g + 1)
            act.activation(avs[:, :], AV[:, 0:L], ACT.Copy).then_inc(sem(f"avs{c}"), 1)

        def weights(u, i, mode):
            if mode != "halve":
                return
            k, c = divmod(u, NG)
            at = slice(c * QW, (c + 1) * QW)
            act.wait_ge(sem("scales"), 1)
            if c == 0:
                wait(act, f"ld_wst{k}", 16 * (i + 1))
                wait(act, f"wr_w{k}", 16 * (i - 8))
            act.activation(w16[k][:, 0, at], wst[k][:, at], ACT.Copy, scale=SC[:, k:k + 1]
                           ).then_inc(sem(f"whi{k}"), 1)

        def step(i, mode):
            for u in range(2 * NG):
                gap(u, 0, i)
                exps(u, 0, i)
                store_weighed(u, i)
                exps(u, 1, i)
                gap(u, 1, i)
                weights(u, i, mode)

        iterations(step, act)

    @block.gpsimd
    def _(pool):
        chain = Chain(pool, sem("pool_chain"), nc, (sem("ones"), 3))
        pool.memset(V[:, :, :, :], 1.0).then_inc(sem("ones"), 1)
        pool.memset(CV[:, :, :], 1.0).then_inc(sem("ones"), 1)
        pool.memset(mhalf[:, :], -0.5).then_inc(sem("ones"), 1)
        pool.wait_ge(sem("ones"), 3)
        pool.wait_ge(sem("ld_rows"), 64)

        def split(n, b):
            if not on(b):
                return
            wait(pool, f"part0_{n}", b + 1)
            chain(pool.tensor_tensor(rest[n][:, :, :], full[n][:, :, :], part[n][:, :, 0, :], ALU.subtract))
            chain(pool.tensor_copy(part[n][:, :, 1, :], rest[n][:, :, :]))
            pool.tensor_tensor(part[n][:, :, 2, :], rest[n][:, :, :], part[n][:, :, 1, :], ALU.subtract
                               ).then_inc(sem(f"parts_{n}"), 1)

        def deviations(c, b):
            if not on(b):
                return
            wait_apart(pool, f"mv{c}", QT * (b + 1), "ones", 3)
            chain(pool.tensor_scalar(ve[:, :], mv[:, :, 1], EPS, None, ALU.add))
            pool.tensor_tensor(rstd[:, :], ve[:, :], mhalf[:, 0:QT], ALU.pow).then_inc(sem(f"rstd{c}"), 1)

        def step(i, mode):
            if mode == "scale":
                pool.wait_ge(sem("wm"), 1)
                pool.partition_all_reduce(wg[:, :], wm[:, :], P, bass.bass_isa.ReduceOp.max
                                          ).then_inc(sem("wg"), 1)
            if on(i):
                wait(pool, "ld_x", 16 * (i + 1))
                wait(pool, "read_O", i)
                pool.tensor_tensor(xbo[:, :, :], xrow[:, :, :],
                                   rows_b[:, 1, :].unsqueeze(1).to_broadcast([P, QT, D]), ALU.add
                                   ).then_inc(sem("xbo"), 1)
            split("q", i + 1)
            split("cq", i - 1)
            deviations("c", i - 2)
            if on(i - 1):
                wait(pool, "x1", i)
                wait(pool, "read_Oc", i - 1)
                pool.tensor_tensor(x1bo[:, :, :], x1s[:, :, :],
                                   rows_b[:, 3, :].unsqueeze(1).to_broadcast([P, QT, D]), ALU.add
                                   ).then_inc(sem("x1bo"), 1)
            split("k", i + 1)
            split("ck", i)
            deviations("", i)

        iterations(step, pool, chain, 4 * 2 + 2)


def experts(nc, ctx, ap, outer, sem):
    ident, identb, mhalf, LG, X2R, SC, b1c, dW, XS, YS = (outer[n] for n in (
        "ident", "identb", "mhalf", "LG", "X2R", "SC", "b1c", "dW", "XS", "YS"))

    def sb(name, shape, dt=F32):
        return ctx.enter_context(nc.sbuf_tensor(name, shape, dt))

    def ps(name, shape, dt=F32):
        return ctx.enter_context(nc.psum_tensor(name, shape, dt))

    W = sb("W", [P, NE, 2, 2, WC], F16)
    b2r = sb("b2r", [P, NE, D])
    tri = sb("tri", [P, P])
    ones = sb("ones2", [P, P])
    ids = sb("ids", [P, NT])
    desc = sb("desc", [P, NE])
    jrow = sb("jrow", [P, NBLK + 1])
    big = [P, NT, NE]
    ex = sb("ex", big)
    pr = sb("pr", big)
    eq = sb("eq", big)
    oh = [sb(f"oh{k}", big) for k in range(2)]
    both = sb("both", big)
    at = sb("at", big)
    cum = sb("cum", [P, NE, NT])
    small = sb("small", [P, 6, NT])
    cnt = sb("cnt", [P, 6, NE])
    cnti = sb("cnti", [P, 2, NE], I32)
    cmp = sb("cmp", [P, NBLK + 1, NE])
    BEf = sb("BEf", [P, NBLK + 1])
    BEi = sb("BEi", [P, NBLK + 1], I32)
    pos = sb("pos", [P, 2, NT])
    posu = sb("posu", [P, 2, NT], U32)
    XB = [sb(f"XB{k}", [P, ROW]) for k in range(2)]
    xhi = sb("xhi", [P, KT, P], F16)
    xlo = sb("xlo", [P, KT, P], F16)
    hhi = [sb(f"hhi{k}", [P, FT, P], F16) for k in range(2)]
    hlo = [sb(f"hlo{k}", [P, FT, P], F16) for k in range(2)]
    wsel = sb("wsel", [P, 4])
    wv = [sb(f"wv{k}", [P, 1]) for k in range(2)]
    tok = [sb(f"tok{k}", [P, 1], U32) for k in range(2)]
    yb = sb("yb", [P, D])
    ysc = [sb(f"ysc{k}", [P, D]) for k in range(2)]
    stats = sb("stats2", [P, 4, 6])
    mv = [sb(f"mv2_{k}", [P, 4, 2]) for k in range(2)]
    ve = sb("ve2", [P, 4])
    rstd = [sb(f"rstd2_{k}", [P, 4]) for k in range(2)]

    HB = [ps(f"HB{k}", [P, 2, 512]) for k in range(2)]
    XTp = ps("XTp", [P, 512])
    YP = ps("YP", [P, 512])
    R0 = ps("R0", [P, 512])
    R1 = ps("R1", [P, 512])
    NS = NT // 4

    block = ctx.enter_context(nc.Block())

    def wait(eng, name, val):
        if not isinstance(val, int) or val > 0:
            eng.wait_ge(sem(name), val)

    def wait_apart(eng, name, val, held, count):
        if not isinstance(val, int) or val > 0:
            apart(nc, eng, sem(name), val, (sem(held), count))

    def blocks(step, eng, chain=None, per=0):
        step(0, 0)
        step(1, 1)
        step(2, 0)
        n = chain.n if chain else 0
        with eng.Fori(0, (NBLK - 5) // 2) as m:
            if chain:
                chain.n, chain.count = n + 2 * per * m, 0
            step(2 * m + 3, 1)
            step(2 * m + 4, 0)
            assert not chain or chain.count == 2 * per, chain.count
        if chain:
            chain.n = n + per * (NBLK - 5)
        step(NBLK - 2, 1)
        step(NBLK - 1, 0)

    assert NBLK % 2 == 1

    @block.sync
    def _(sp):
        for dst, name in ((ids[:, :], "ids"), (tri[:, :], "tri"), (desc[:, :], "desc"), (jrow[:, :], "jrow")):
            sp.dma_start(dst, ap[name]).then_inc(sem("ld_route"), 16)
        sp.dma_start(b2r[:, :, :].rearrange("p e d -> p (e d)"),
                     ap["b2"].rearrange("e d -> (e d)").partition_broadcast(P)).then_inc(sem("ld_b2"), 16)
        sp.dma_start(W[:, 0].rearrange("p a c n -> p (a c n)"), dW[0].rearrange("p a c n -> p (a c n)")
                     ).then_inc(sem("ld_W"), 16)

        def load_rows(j, q):
            sp.dma_start(XB[q][:, :], XS.rearrange("(j p) c -> j p c", p=P)[bass.ds(j, 1)]
                         .rearrange("j p c -> p (j c)")).then_inc(sem("ld_XB"), 16)

        sp.wait_ge(sem("scatter"), 16 * 2 * NT)
        load_rows(0, 0)
        for e in range(1, NE):
            sp.wait_ge(sem("ld_W"), 16 * e)
            sp.dma_start(W[:, e].rearrange("p a c n -> p (a c n)"), dW[e].rearrange("p a c n -> p (a c n)")
                         ).then_inc(sem("ld_W"), 16)
            if e == 1:
                sp.wait_ge(sem("ld_XB"), 16)
                load_rows(1, 1)

        def step(j, q):
            if isinstance(j, int) and j + 2 >= NBLK:
                return
            wait(sp, "XT", j + 1)
            wait(sp, "wv", j + 1)
            wait(sp, "tok", j + 1)
            wait(sp, "ld_XB", 16 * (j + 2))
            load_rows(j + 2, q)

        blocks(step, sp)
        sp.wait_ge(sem("add"), 16 * NBLK)
        rows = YS[0:T, :].rearrange("(t p) d -> p t d", p=P)
        for s in range(NS):
            sp.dma_start(X2R[:, 4 * s:4 * s + 4, 0:D], rows[:, 4 * s:4 * s + 4, :]).then_inc(sem(f"ld_Y{s}"), 16)
        for s in range(NS):
            sp.wait_ge(sem("fin"), s + 1)
            sp.dma_start(ap["out"].rearrange("(t p) d -> p t d", p=P)[:, 4 * s:4 * s + 4, :],
                         X2R[:, 4 * s:4 * s + 4, 0:D]).then_inc(sem("wr_out"), 16)
        sp.wait_ge(sem("wr_out"), 16 * NS)

    @block.tensor
    def _(pe):
        pe.wait_ge(sem("ld_route"), 64)
        pe.wait_ge(sem("ones_r"), 1)
        pe.wait_ge(sem("both"), 1)
        flat = both[:, :, :].rearrange("p t e -> p (t e)")
        pe.matmul(R0[:, 0:NT * NE], tri[:, :], flat, start=True, stop=True)
        pe.matmul(R1[:, 0:NT * NE], ones[:, :], flat, start=True, stop=True).then_inc(sem("counts"), 1)

        def turn(j, q):
            wait(pe, "ld_XB", 16 * (j + 1))
            wait(pe, "xlo", j)
            for k in range(KT):
                mm = pe.transpose(XTp[:, k * P:(k + 1) * P], XB[q][:, k * P:(k + 1) * P], ident[:, :])
            mm.then_inc(sem("XT"), 1)

        def expert_of(j):
            return pe.value_load(BEi[0:1, bass.ds(j, 1)], min_val=0, max_val=NE - 1)

        def first(j, q):
            e = expert_of(j)
            pe.wait_ge(sem("ld_W"), 16 * e + 16)
            wait(pe, "xlo", j + 1)
            wait(pe, "hlo", 2 * (j - 1) if isinstance(j, int) else 2 * (j - 1))
            for f in range(FT):
                out = HB[q][:, f // 4, (f % 4) * P:(f % 4 + 1) * P]
                n = 0
                for half, x in ((0, xhi), (0, xlo), (1, xhi)):
                    for k in range(KT):
                        w = W[:, bass.ds(e, 1), 0, half, k * F + f * P:k * F + (f + 1) * P]
                        mm = pe.matmul(out, w.rearrange("p e n -> p (e n)"), x[:, k, :],
                                       start=(n == 0), stop=(n == 5))
                        n += 1
                if f % 4 == 3:
                    mm.then_inc(sem("HB"), 1)

        def second(j, q):
            e = expert_of(j)
            wait(pe, "hlo", 2 * (j + 1))
            wait(pe, "yb", j)
            n = 0
            for f in range(FT):
                for half, h in ((0, hhi), (0, hlo), (1, hhi)):
                    w = W[:, bass.ds(e, 1), 1, half, f * D:(f + 1) * D]
                    mm = pe.matmul(YP[:, 0:D], h[q][:, f, :], w.rearrange("p e n -> p (e n)"),
                                   start=(n == 0), stop=(n == 3 * FT - 1))
                    n += 1
            mm.then_inc(sem("YP"), 1)

        pe.wait_ge(sem("table"), 1)

        def step(j, q):
            if isinstance(j, int) and j == 0:
                turn(0, 0)
            first(j, q)
            if not (isinstance(j, int) and j == NBLK - 1):
                turn(j + 1, 1 - q)
            if not (isinstance(j, int) and j == 0):
                second(j - 1, 1 - q)

        blocks(step, pe)
        second(NBLK - 1, (NBLK - 1) % 2)

    @block.scalar
    def _(act):
        act.wait_ge(sem("centred"), 1)
        act.activation(ex[:, :, :], eq[:, :, :], ACT.Exp).then_inc(sem("ex"), 1)

        def xhalf(j):
            wait(act, "XT", j + 1)
            if not (isinstance(j, int) and j == 0):
                wait(act, "HB", 2 * j)
            act.activation(xhi[:, :, :], XTp[:, 0:D].rearrange("p (k n) -> p k n", k=KT), ACT.Copy
                           ).then_inc(sem("xhi"), 1)

        def hidden(j, q):
            if not (isinstance(j, int) and j < 2):
                wait(act, "YP", j - 1)
            for c in range(2):
                wait(act, "hid", 2 * j + c + 1)
                act.activation(hhi[q][:, 4 * c:4 * c + 4, :].rearrange("p f n -> p (f n)"), HB[q][:, c, :],
                               ACT.Relu).then_inc(sem("hhi"), 1)

        def weigh(j, q):
            wait(act, "yb", j + 1)
            wait(act, "wv", j + 1)
            if not (isinstance(j, int) and j < 2):
                wait(act, "add", 16 * (j - 1))
            act.activation(ysc[q][:, :], yb[:, :], ACT.Copy, scale=wv[q][:, 0:1]).then_inc(sem("ysc"), 1)

        def step(j, q):
            if isinstance(j, int) and j == 0:
                xhalf(0)
            hidden(j, q)
            if not (isinstance(j, int) and j == NBLK - 1):
                xhalf(j + 1)
            if not (isinstance(j, int) and j == 0):
                weigh(j - 1, 1 - q)

        blocks(step, act)
        weigh(NBLK - 1, (NBLK - 1) % 2)

    @block.vector
    def _(dve):
        chain = Chain(dve, sem("dve_chain2"))

        def bc(t):
            return t.unsqueeze(2).to_broadcast([P, NT, NE])

        dve.memset(ones[:, :], 1.0).then_inc(sem("ones_r"), 1)
        dve.wait_ge(sem("ld_route"), 64)
        top, den, rden, w1, w2, best = (small[:, n, :] for n in range(6))
        chain(dve.tensor_reduce(top, LG[:, :, :], AX.X, ALU.max))
        dve.tensor_tensor(eq[:, :, :], LG[:, :, :], bc(top), ALU.subtract).then_inc(sem("centred"), 1)
        dve.wait_ge(sem("ex"), 1)
        chain(dve.tensor_reduce(den, ex[:, :, :], AX.X, ALU.add))
        chain(dve.reciprocal(rden, den))
        chain(dve.tensor_tensor(pr[:, :, :], ex[:, :, :], bc(rden), ALU.mult))
        for k, w in ((0, w1), (1, w2)):
            chain(dve.tensor_reduce(w, pr[:, :, :], AX.X, ALU.max))
            chain(dve.tensor_tensor(eq[:, :, :], pr[:, :, :], bc(w), ALU.is_equal))
            chain(dve.tensor_tensor(eq[:, :, :], eq[:, :, :],
                                    desc[:, :].unsqueeze(1).to_broadcast([P, NT, NE]), ALU.mult))
            chain(dve.tensor_reduce(best, eq[:, :, :], AX.X, ALU.max))
            chain(dve.tensor_tensor(oh[k][:, :, :], eq[:, :, :], bc(best), ALU.is_equal))
            if k == 0:
                chain(dve.tensor_scalar(X2R[:, :, D + 3], best, -1.0, float(NE), ALU.mult, ALU.add))
                chain(dve.tensor_scalar(eq[:, :, :], oh[0][:, :, :], -2.0, None, ALU.mult))
                chain(dve.tensor_tensor(pr[:, :, :], pr[:, :, :], eq[:, :, :], ALU.add))
        chain(dve.tensor_copy(X2R[:, :, D], w1))
        chain(dve.tensor_copy(X2R[:, :, D + 2], ids[:, :]))
        chain(dve.tensor_copy(X2R[:, :, D + 1], w2))
        dve.tensor_tensor(both[:, :, :], oh[0][:, :, :], oh[1][:, :, :], ALU.add).then_inc(sem("both"), 1)
        dve.wait_ge(sem("counts"), 1)
        tot = R1[:, 0:NT * NE].rearrange("p (t e) -> p t e", e=NE)
        for e in range(NE):
            ins = dve.tensor_tensor_scan(cum[:, e, :], ones[:, 0:NT], tot[:, :, e], 0.0, ALU.mult, ALU.add)
            chain(ins)
        n, n127, nb, cb, base, _ = (cnt[:, k, :] for k in range(6))
        chain(dve.tensor_copy(n, cum[:, :, NT - 1]))
        chain(dve.tensor_tensor(at[:, :, :], cum[:, :, :].rearrange("p e t -> p t e"), tot, ALU.subtract))
        chain(dve.tensor_tensor(at[:, :, :], at[:, :, :], R0[:, 0:NT * NE].rearrange("p (t e) -> p t e", e=NE),
                                ALU.add))
        chain(dve.tensor_scalar(n127, n, float(P - 1), None, ALU.add))
        chain(dve.tensor_copy(cnti[:, 0, :], n127))
        chain(dve.tensor_scalar(cnti[:, 1, :], cnti[:, 0, :], 7, None, ALU.arith_shift_right))
        chain(dve.tensor_copy(nb, cnti[:, 1, :]))
        chain(dve.tensor_tensor_scan(cb, ones[:, 0:NE], nb, 0.0, ALU.mult, ALU.add))
        chain(dve.tensor_tensor(base, cb, nb, ALU.subtract))
        chain(dve.tensor_scalar(base, base, float(P), None, ALU.mult))
        chain(dve.tensor_tensor(at[:, :, :], at[:, :, :], base.unsqueeze(1).to_broadcast([P, NT, NE]), ALU.add))
        for k in range(2):
            chain(dve.tensor_tensor(eq[:, :, :], at[:, :, :], oh[k][:, :, :], ALU.mult))
            chain(dve.tensor_reduce(pos[:, k, :], eq[:, :, :], AX.X, ALU.add))
        dve.tensor_copy(posu[:, :, :], pos[:, :, :]).then_inc(sem("posu"), 1)
        chain(dve.tensor_tensor(cmp[:, :, :], jrow[:, :].unsqueeze(2).to_broadcast([P, NBLK + 1, NE]),
                                cb.unsqueeze(1).to_broadcast([P, NBLK + 1, NE]), ALU.is_ge))
        chain(dve.tensor_reduce(BEf[:, :], cmp[:, :, :], AX.X, ALU.add))
        chain(dve.tensor_scalar(BEf[:, :], BEf[:, :], float(NE - 1), None, ALU.min))
        dve.tensor_copy(BEi[:, :], BEf[:, :]).then_inc(sem("table"), 1)
        dve.wait_ge(sem("table"), 1)

        def expert_of(j):
            return dve.value_load(BEi[0:1, bass.ds(j, 1)], min_val=0, max_val=NE - 1)

        def xhalf(j):
            wait(dve, "xhi", j + 1)
            dve.tensor_tensor(xlo[:, :, :], XTp[:, 0:D].rearrange("p (k n) -> p k n", k=KT), xhi[:, :, :],
                              ALU.subtract).then_inc(sem("xlo"), 1)

        def hidden(j, q, e, c):
            bank = HB[q][:, c, :].rearrange("p (f n) -> p f n", n=P)
            wait(dve, "HB", 2 * j + c + 1)
            dve.scalar_tensor_tensor(bank, bank, SC[:, 3:4],
                                     b1c[:, bass.ds(e, 1), 4 * c:4 * c + 4].rearrange("p e f -> p (e f)")
                                     .unsqueeze(2).to_broadcast([P, 4, P]), ALU.mult, ALU.add
                                     ).then_inc(sem("hid"), 1)

        def low(j, q, c):
            wait(dve, "hhi", 2 * j + c + 1)
            dve.scalar_tensor_tensor(hlo[q][:, 4 * c:4 * c + 4, :].rearrange("p f n -> p (f n)"), HB[q][:, c, :],
                                     0.0, hhi[q][:, 4 * c:4 * c + 4, :].rearrange("p f n -> p (f n)"),
                                     ALU.max, ALU.subtract).then_inc(sem("hlo"), 1)

        def weights(j, q):
            if not (isinstance(j, int) and j < 2):
                wait(dve, "ysc", j - 1)
            wait(dve, "ld_XB", 16 * (j + 1))
            of = BEf[:, bass.ds(j, 1)]
            e1 = XB[q][:, D + 3:D + 4]
            dve.tensor_scalar(wsel[:, 0:1], e1, of, XB[q][:, D:D + 1], ALU.is_equal, ALU.mult)
            chain(dve.tensor_scalar(wsel[:, 1:2], e1, of, XB[q][:, D + 1:D + 2], ALU.not_equal, ALU.mult))
            dve.tensor_tensor(wv[q][:, :], wsel[:, 0:1], wsel[:, 1:2], ALU.add).then_inc(sem("wv"), 1)

        def result(j, q):
            e = expert_of(j)
            wait(dve, "YP", j + 1)
            wait(dve, "ysc", j)
            dve.scalar_tensor_tensor(yb[:, :], YP[:, 0:D], SC[:, 4:5],
                                     b2r[:, bass.ds(e, 1), :].rearrange("p e d -> p (e d)"),
                                     ALU.mult, ALU.add).then_inc(sem("yb"), 1)

        def step(j, q):
            if isinstance(j, int) and j == 0:
                dve.wait_ge(sem("ld_b2"), 16)
                xhalf(0)
            weights(j, q)
            e = expert_of(j)
            hidden(j, q, e, 0)
            hidden(j, q, e, 1)
            low(j, q, 0)
            low(j, q, 1)
            if not (isinstance(j, int) and j == NBLK - 1):
                xhalf(j + 1)
            if not (isinstance(j, int) and j == 0):
                result(j - 1, 1 - q)

        blocks(step, dve, chain, 1)
        result(NBLK - 1, (NBLK - 1) % 2)

        def moments(s):
            q = s % 2
            dve.wait_ge(sem(f"ld_Y{s}"), 16)
            if s:
                dve.wait_ge(sem("mom"), s)
            for t in range(4):
                ins = dve.bn_stats(stats[:, t, :], X2R[:, 4 * s + t, 0:D])
            chain(ins)
            for t in range(4):
                ins = dve.bn_aggr(mv[q][:, t, :], stats[:, t, :])
            ins.then_inc(sem("mom"), 1)

        def normalise(s):
            q = s % 2
            dve.wait_ge(sem("dev"), s + 1)
            for t in range(4):
                ins = dve.tensor_scalar(X2R[:, 4 * s + t, 0:D], X2R[:, 4 * s + t, 0:D], mv[q][:, t, 0:1],
                                        rstd[q][:, t:t + 1], ALU.subtract, ALU.mult)
            ins.then_inc(sem("fin"), 1)

        for s in range(NS):
            moments(s)
            if s:
                normalise(s - 1)
        normalise(NS - 1)

    @block.gpsimd
    def _(pool):
        chain = Chain(pool, sem("pool_chain2"))
        pool.wait_ge(sem("posu"), 1)
        for t in range(NT):
            for k in range(2):
                pool.indirect_dma_start(XS, bass.IndirectOffsetOnAxis(ap=posu[:, k, t:t + 1], axis=0),
                                        X2R[:, t, :], None).then_inc(sem("scatter"), 16)

        def number(j, q):
            if not (isinstance(j, int) and j < 2):
                wait(pool, "add", 16 * (j - 1))
            wait_apart(pool, "ld_XB", 16 * (j + 1), "posu", 1)
            pool.tensor_copy(tok[q][:, :], XB[q][:, D + 2:D + 3]).then_inc(sem("tok"), 1)

        def add(j, q):
            wait_apart(pool, "ysc", j + 1, "posu", 1)
            wait(pool, "tok", j + 1)
            wait(pool, "add", 16 * j)
            pool.indirect_dma_start(YS, bass.IndirectOffsetOnAxis(ap=tok[q][:, 0:1], axis=0),
                                    ysc[q][:, :], None, compute_op=ALU.add).then_inc(sem("add"), 16)

        def step(j, q):
            number(j, q)
            if not (isinstance(j, int) and j == 0):
                add(j - 1, 1 - q)

        blocks(step, pool)
        add(NBLK - 1, (NBLK - 1) % 2)
        for s in range(NS):
            q = s % 2
            pool.wait_ge(sem("mom"), s + 1)
            if s >= 2:
                pool.wait_ge(sem("fin"), s - 1)
            if s:
                pool.wait_ge(sem("dev"), s)
            chain(pool.tensor_scalar(ve[:, :], mv[q][:, :, 1], EPS, None, ALU.add))
            pool.tensor_tensor(rstd[q][:, :], ve[:, :], mhalf[:, :], ALU.pow).then_inc(sem("dev"), 1)


def _bf16_parts(a):
    out = []
    for _ in range(PARTS):
        u = a.astype(np.float32).view(np.uint32).astype(np.uint64)
        r = ((u + 0x7FFF + ((u >> 16) & 1)) & 0xFFFF0000).astype(np.uint32).view(np.float32)
        out.append(r)
        a = a - r
    return out


def _aux(n, bias):
    q = np.zeros((AUX, H, n), np.float32)
    k = np.zeros((AUX, H, n), np.float32)
    q[0:PARTS] = 1.0
    if bias is not None:
        k[0:PARTS] = np.stack(_bf16_parts(bias))
    for a in range(PARTS):
        for h in range(H):
            k[PARTS + GH * a + h % GH, h] = 1.0
    return q, k


def kernel(**inputs):
    import concourse.bacc as _bacc
    from concourse.bass_utils import run_bass_kernel_spmd as _run

    g = {k: np.asarray(v) for k, v in inputs.items()}
    order = np.arange(D).reshape(KT, HM, HD).transpose(0, 2, 1).reshape(D)

    def col(b):
        return np.ascontiguousarray(b[order].reshape(KT, P).T)

    slopes = np.power(np.float32(2.0), np.linspace(-4.0, -0.3, H).astype(np.float32)).astype(np.float32)
    alibi = -(slopes[:, None] * np.arange(L, dtype=np.float32)[None, :])
    aux_q, aux_k = _aux(L, alibi)
    aux_cq, _ = _aux(L, None)
    _, aux_ck = _aux(LC, None)
    fill = np.zeros((P, ROW), np.float32)
    fill[:, D + 2] = T + np.arange(P)
    arrays = dict(
        x=g["x"], xT=g["x"].transpose(0, 2, 1), ctxT=g["ctx_1024"].transpose(0, 2, 1),
        mask=g["mask_Bx1x1xS2_fk0"].reshape(B, LC),
        wq=g["L0_attn_Wq"].T[:, order], wk=g["L0_attn_Wk"].T[:, order], wv=g["L0_attn_Wv"].T, wo=g["L0_attn_Wo"].T,
        cwq=g["L0_xattn_Wq"][:, order], cwk=g["L0_xattn_Wk"][:, order], cwv=g["L0_xattn_Wv"], cwo=g["L0_xattn_Wo"],
        bq=col(g["L0_attn_bq"]), bk=col(g["L0_attn_bk"]), cbq=col(g["L0_xattn_bq"]), cbk=col(g["L0_xattn_bk"]),
        bv=g["L0_attn_bv"], bo=g["L0_attn_bo"], cbv=g["L0_xattn_bv"], cbo=g["L0_xattn_bo"],
        gate=g["L0_ffn_gate_w"].T,
        w1=g["L0_ffn_w1"], w2=g["L0_ffn_w2"], b2=g["L0_ffn_b2"],
        b1t=g["L0_ffn_b1"].reshape(NE, FT, P).transpose(2, 0, 1),
        fill=fill, ids=np.arange(T, dtype=np.float32).reshape(NT, P).T,
        tri=np.triu(np.ones((P, P), np.float32), 1),
        desc=np.tile(np.arange(NE, 0, -1, dtype=np.float32), (P, 1)),
        jrow=np.tile(np.arange(NBLK + 1, dtype=np.float32), (P, 1)),
        ident=np.eye(P, dtype=np.float32), aux_q=aux_q, aux_k=aux_k, aux_cq=aux_cq, aux_ck=aux_ck)
    nc = _bacc.Bacc("TRN2", target_bir_lowering=False, num_devices=1)
    feeds, ap = {}, {}
    for name, a in arrays.items():
        a = np.ascontiguousarray(a)
        feeds[f"in_{name}"] = a
        ap[name] = nc.dram_tensor(f"in_{name}", a.shape, mybir.dt.from_np(a.dtype), kind="ExternalInput").ap()
    ap["out"] = nc.dram_tensor("out_y", (T, D), F32, kind="ExternalOutput").ap()
    emit(nc, ap)
    r = _run(nc, [feeds], core_ids=[0])
    return r.results[0]["out_y"].reshape(B, L, D)
```

```python
from contextlib import ExitStack

import numpy as np

import concourse.bass as bass
from concourse import mybir

ALU = mybir.AluOpType
ACT = mybir.ActivationFunctionType
AX = mybir.AxisListType
F32 = mybir.dt.float32
BF16 = mybir.dt.bfloat16
F16 = mybir.dt.float16
I32 = mybir.dt.int32
U32 = mybir.dt.uint32
U16 = mybir.dt.uint16

P = 128
B, L, D = 16, 256, 256
LC = 120
H, HD = 16, 16
NE, F = 8, 1024
T = B * L
KT = D // P
QT = L // P
HM = H // KT
NG = 4
GH = H // NG
PROD = 96
AUX = 15
PARTS = 3
NT = T // P
NBLK = 2 * T // P + NE - 1
ROW = D + 4
FT = F // P
WC = KT * F
SQ = 1.0 / float(np.sqrt(HD))
EPS = 1e-5
Q_RUNS = [(0, 0, 3), (3, 0, 2), (5, 0, 1)]
K_BLOCKS = [0, 0, 0, 1, 1, 2]


class Chain:

    def __init__(self, eng, sem, nc=None, held=None):
        self.nc, self.eng, self.sem, self.held, self.n, self.count = nc, eng, sem, held, 0, 0

    def put(self, ins):
        ins.then_inc(self.sem, 1)
        self.n = self.n + 1
        self.count += 1

    def wait(self):
        if self.held:
            apart(self.nc, self.eng, self.sem, self.n, self.held)
        else:
            self.eng.wait_ge(self.sem, self.n)

    def __call__(self, ins):
        self.put(ins)
        self.wait()


def apart(nc, eng, sem, value, held):
    value = value if isinstance(value, int) else nc.snap(value)
    eng.wait_ge(*held)
    eng.wait_ge(sem, value)


def emit(nc, ap):
    ctx = ExitStack()
    with ctx:
        build(nc, ctx, ap)


def build(nc, ctx, ap):
    def sb(name, shape, dt=F32):
        return ctx.enter_context(nc.sbuf_tensor(name, shape, dt))

    sems = {}

    def sem(name):
        if name not in sems:
            sems[name] = ctx.enter_context(nc.semaphore(name))
        return sems[name]

    ident = sb("ident", [P, P])
    identb = sb("identb", [P, P], BF16)
    mhalf = sb("mhalf", [P, 4])
    LG = sb("LG", [P, NT, NE])
    X2R = sb("X2R", [P, NT, ROW])
    SC = sb("SC", [P, 5])
    b1c = sb("b1c", [P, NE, FT])
    dW = nc.dram_tensor("d_w", [NE, P, 2, 2, WC], F16).ap()
    XS = nc.dram_tensor("d_rows", [NBLK * P, ROW], F32).ap()
    YS = nc.dram_tensor("d_sums", [T + P, D], F32).ap()
    outer = dict(ident=ident, identb=identb, mhalf=mhalf, LG=LG, X2R=X2R, SC=SC, b1c=b1c, dW=dW, XS=XS, YS=YS)
    with ExitStack() as inner:
        attention(nc, inner, ap, outer, sem)
    with ExitStack() as inner:
        experts(nc, inner, ap, outer, sem)


def attention(nc, ctx, ap, outer, sem):
    ident, identb, mhalf, LG, X2R, SC, b1c, dW, XS, YS = (outer[n] for n in (
        "ident", "identb", "mhalf", "LG", "X2R", "SC", "b1c", "dW", "XS", "YS"))

    def sb(name, shape, dt=F32):
        return ctx.enter_context(nc.sbuf_tensor(name, shape, dt))

    def ps(name, shape, dt=F32):
        return ctx.enter_context(nc.psum_tensor(name, shape, dt))

    wq, wk, wv, wo = (sb(n, [P, KT, D]) for n in ("wq", "wk", "wv", "wo"))
    cq, ck, cv, co = (sb(n, [P, KT, D]) for n in ("cq", "ck", "cv", "co"))
    cols = sb("cols", [P, 4, KT])
    rows_b = sb("rows_b", [P, 4, D])
    maskt = sb("maskt", [B, LC])
    maskr = sb("maskr", [B, 2, LC])
    maskp = sb("maskp", [B, PARTS, LC], BF16)

    xT = sb("xT", [P, KT, L])
    cT = sb("cT", [P, KT, LC])
    xrow = sb("xrow", [P, QT, D])
    xbo = sb("xbo", [P, QT, D])
    x1T = sb("x1T", [P, KT, L])
    names = ("q", "k", "cq", "ck")
    width = dict(q=L, k=L, cq=L, ck=LC)
    full = {n: sb(f"{n}_full", [P, KT, width[n]]) for n in names}
    rest = {n: sb(f"{n}_rest", [P, KT, width[n]]) for n in names}
    part = {n: sb(f"{n}_part", [P, KT, PARTS, width[n]], BF16) for n in names}
    stack = {n: sb(f"{n}_stack", [PROD + AUX, H, width[n]], BF16) for n in names}
    V = sb("V", [P, QT, H, 2 * HD])
    CV = sb("CV", [P, H, 2 * HD])
    PT = sb("PT", [P, 2, GH, 2, L])
    mneg = sb("mneg", [P, QT, GH])
    mr = sb("mr", [P, QT, GH])
    MTp = sb("MTp", [P, QT, 16], BF16)
    mts = sb("mts", [16, L], BF16)
    avs = sb("avs", [P, L])
    rc = sb("rc", [P, QT, GH])
    ao = sb("ao", [P, QT, D])
    aoT = sb("aoT", [P, KT, L])
    r1 = sb("r1", [P, QT, D])
    stats = sb("stats", [P, QT, 6])
    mv = sb("mv", [P, QT, 2])
    ve = sb("ve", [P, QT])
    rstd = sb("rstd", [P, QT])
    shift = sb("shift", [P, QT])
    minus = sb("minus", [P, QT + 1])
    x1s = sb("x1s", [P, QT, D])
    x1bo = sb("x1bo", [P, QT, D])
    x2s = sb("x2s", [P, QT, D])
    x2T = sb("x2T", [P, KT, L])
    gate = sb("gate", [P, KT, NE])
    wst = [sb(f"wst{k}", [P, WC]) for k in range(2)]
    w16 = [sb(f"w16_{k}", [P, 2, WC], F16) for k in range(2)]
    wmx = sb("wmx", [P, 2, NG, NE])
    wm = sb("wm", [P, 3])
    wg = sb("wg", [P, 3])
    wp = sb("wp", [P, 8])
    b1t = sb("b1t", [P, NE, FT])
    fill = sb("fill", [P, ROW])

    SA = ps("SA", [P, 2, 512])
    SB = ps("SB", [P, 2, 512])
    AV = ps("AV", [P, 512])
    MT = ps("MT", [16, 1024], BF16)
    BK = [ps("BK0", [P, 512]), ps("BK1", [P, 512])]

    dpart = {n: nc.dram_tensor(f"d_{n}", [KT, PARTS, P, width[n]], BF16).ap() for n in names}
    dmask = nc.dram_tensor("d_mask", [B, PARTS, LC], BF16).ap()

    def half_of(k, half, c):
        if k == 0:
            return w16[0][:, half, c * QW:(c + 1) * QW]
        both = w16[1][:, :, :].rearrange("p a n -> p (a n)").rearrange("p (f a d) -> p f a d", a=2, d=D)
        return both[:, c * QW // D:(c + 1) * QW // D, half, :]

    def quarter(k, c):
        w = wst[k][:, c * QW:(c + 1) * QW]
        return w if k == 0 else w.rearrange("p (f d) -> p f d", d=D)

    def on(b):
        return not isinstance(b, int) or 0 <= b < B

    def wait(eng, name, val):
        if not isinstance(val, int) or val > 0:
            eng.wait_ge(sem(name), val)

    def wait_apart(eng, name, val, held, count):
        if not isinstance(val, int) or val > 0:
            apart(nc, eng, sem(name), val, (sem(held), count))

    ITEMS = [[("Q", 1), ("T1", -1), ("AOTc", -2), ("Kc", 0), ("T2", -2), ("AOT", 0)],
             [("Qc", -1), ("Vc", -1), ("Oc", -2), ("K", 1), ("V", 1), ("O", 0), ("R", -2)]]
    BANK = {n: k for k in range(2) for n, _ in ITEMS[k]}

    def bank_free(eng, name, i):
        order = ITEMS[BANK[name]]
        at = [n for n, _ in order].index(name)
        for back in range(1, 14):
            pos = at - back
            n, off = order[pos % len(order)]
            b = i + off + pos // len(order)
            if on(b):
                wait(eng, f"read_{n}", b + 1)
                return

    def iterations(step, eng, chain=None, per=0):
        for i in (-1, 0, 1, 2):
            step(i, "max")
        looped(step, eng, 3, 6, "max", chain, per)
        step(6, "max")
        step(7, "scale")
        step(8, "halve")
        looped(step, eng, 9, B - 2, "halve", chain, per)
        step(B - 2, "halve")
        step(B - 1, "halve")
        step(B, None)
        step(B + 1, None)

    def looped(step, eng, first, end, mode, chain, per):
        n = chain.n if chain else 0
        with eng.Fori(first, end) as i:
            if chain:
                chain.n, chain.count = n + per * (i - first), 0
            step(i, mode)
            assert not chain or chain.count == per, chain.count
        if chain:
            chain.n = n + per * (end - first)

    def group(u, i, back):
        n = u - back
        if n < 0:
            n, i = n + 2 * NG, i - 1
        return (True, i, n) if n < NG else (False, i - 1, n - NG)

    def last(eng, u, i, back, what, per=1):
        for more in range(8):
            if u - back - more < -8:
                return
            mine, b, g = group(u, i, back + more)
            if on(b):
                n = per if mine else 1
                wait(eng, what + ("" if mine else "c"), n * (NG * b + g + 1))
                return

    GAPS = {(0, 0): ("Q", 1), (0, 1): ("T1", -1), (1, 0): ("Qc", -1), (2, 0): ("Vc", -1),
            (2, 1): ("AOTc", -2), (3, 1): ("Oc", -2), (4, 0): ("K", 1), (4, 1): ("Kc", 0),
            (5, 1): ("V", 1), (6, 0): ("T2", -2), (6, 1): ("AOT", 0), (7, 0): ("O", 0), (7, 1): ("R", -2)}

    block = ctx.enter_context(nc.Block())

    N_Q, N_K = len(Q_RUNS), len(K_BLOCKS)
    FILL_STEPS = (0, 1, 2, 6, 7)
    FILL = -(-NBLK // len(FILL_STEPS))
    QW = WC // NG

    @block.sync
    def _(sp):
        for dst, src in ((wq, "wq"), (wk, "wk"), (wv, "wv")):
            sp.dma_start(dst[:, :, :], ap[src].rearrange("(k p) n -> p k n", p=P)).then_inc(sem("ld_w"), 16)
        sp.dma_start(xT[:, :, :], ap["xT"][0].rearrange("(k p) n -> p k n", p=P)).then_inc(sem("ld_xT"), 16)
        for n, name in enumerate(("bq", "bk", "cbq", "cbk")):
            sp.dma_start(cols[:, n, :], ap[name]).then_inc(sem("ld_cols"), 16)
        for n, name in enumerate(("bv", "bo", "cbv", "cbo")):
            sp.dma_start(rows_b[:, n, :], ap[name].partition_broadcast(P)).then_inc(sem("ld_rows"), 16)
        sp.dma_start(cT[:, :, :], ap["ctxT"][0].rearrange("(k p) n -> p k n", p=P)).then_inc(sem("ld_cT"), 16)
        sp.dma_start(maskt[:, :], ap["mask"]).then_inc(sem("ld_mask"), 16)
        sp.dma_start(ident[:, :], ap["ident"]).then_inc(sem("ld_const"), 16)
        sp.dma_start(gate[:, :, :], ap["gate"].rearrange("(k p) n -> p k n", p=P)).then_inc(sem("ld_gate"), 16)
        for name in names:
            sp.dma_start(stack[name][PROD:PROD + AUX, :, :].bitcast(U16), ap[f"aux_{name}"]
                         ).then_inc(sem("aux_set"), 16)
        for dst, src in ((wo, "wo"), (cq, "cwq"), (ck, "cwk"), (cv, "cwv"), (co, "cwo")):
            sp.dma_start(dst[:, :, :], ap[src].rearrange("(k p) n -> p k n", p=P)).then_inc(sem("ld_w2"), 16)
        sp.dma_start(fill[:, :], ap["fill"]).then_inc(sem("ld_fill"), 16)
        sp.dma_start(b1t[:, :, :], ap["b1t"]).then_inc(sem("ld_b1"), 16)

        def write_parts(n, b):
            wait(sp, f"parts_{n}", b + 1)
            sp.dma_start(dpart[n].rearrange("k a p t -> p (k a) t"),
                         part[n][:, :, :, :].rearrange("p k a t -> p (k a) t")).then_inc(sem(f"wr_{n}"), 16)

        def read_stack(n, b, blocks):
            wait(sp, f"wr_{n}", (b + 1) * 16)
            for block0, part0, count in blocks:
                src = dpart[n].rearrange("k a (d m) t -> k (a d) (m t)", m=HM)
                src = src[:, part0 * HD:(part0 + count) * HD, :].rearrange("k p n -> p k n")
                dst = stack[n][block0 * HD:(block0 + count) * HD, :, :].rearrange(
                    "p (k m) t -> p k (m t)", k=KT)
                sp.dma_start(dst, src).then_inc(sem(f"st_{n}"), 16)

        k_runs = [(n, a, 1) for n, a in enumerate(K_BLOCKS)]

        def load_expert(e, k):
            src = (ap["w1"] if k == 0 else ap["w2"])[bass.ds(e, 1)]
            sp.dma_start(wst[k][:, :].rearrange("p (a n) -> p a n", a=KT if k == 0 else FT),
                         src.rearrange("e (a p) n -> p (e a) n", p=P)).then_inc(sem(f"ld_wst{k}"), 16)

        def experts_in(i, mode, k):
            if mode == "max":
                wait(sp, f"wmax{k}", i + 1)
                load_expert(i + 1, k)
            elif mode == "halve":
                load_expert(i - 8, k)

        def experts_out(i, mode, k):
            if mode == "halve":
                wait(sp, f"wlo{k}", i - 7)
                sp.dma_start(dW[bass.ds(i - 8, 1), :, k].rearrange("e p a n -> p (e a) n"),
                             w16[k][:, :, :]).then_inc(sem(f"wr_w{k}"), 16)

        def fill_rows(i):
            if not isinstance(i, int) or i not in FILL_STEPS:
                return
            n = FILL_STEPS.index(i)
            sp.wait_ge(sem("ld_fill"), 16)
            here = slice(n * FILL, min((n + 1) * FILL, NBLK))
            sp.dma_start(XS.rearrange("(j p) c -> p j c", p=P)[:, here],
                         fill[:, :].unsqueeze(1).to_broadcast([P, here.stop - here.start, ROW])
                         ).then_inc(sem("wr_fill"), 16)
            if n == 0:
                sp.dma_start(YS[T:T + P, :], fill[:, 0:D]).then_inc(sem("wr_fill"), 16)

        def step(i, mode):
            experts_in(i, mode, 1)
            if on(i):
                wait(sp, "xbo", i)
                sp.dma_start(xrow[:, :, :], ap["x"][bass.ds(i, 1)].rearrange("b (t p) d -> p (b t) d", p=P)
                             ).then_inc(sem("ld_x"), 16)
            if on(i - 1):
                wait_apart(sp, "STc", NG * (i - 1), "wr_mask", 16)
                read_stack("ck", i - 1, k_runs)
                sp.dma_start(stack["ck"][PROD:PROD + PARTS, :, :],
                             dmask[bass.ds(i - 1, 1)].rearrange("b a t -> (b a) t").unsqueeze(1)
                             .to_broadcast([PARTS, H, LC])).then_inc(sem("st_ck"), 16)
                write_parts("cq", i - 1)
                read_stack("cq", i - 1, Q_RUNS)
            if on(i + 1):
                write_parts("q", i + 1)
            if on(i) and not (isinstance(i, int) and i == 0):
                wait(sp, "Vc", i)
                sp.dma_start(cT[:, :, :], ap["ctxT"][bass.ds(i, 1)].rearrange("b (k p) n -> p (b k) n", p=P)
                             ).then_inc(sem("ld_cT"), 16)
            if on(i + 1):
                write_parts("k", i + 1)
                wait_apart(sp, "ST", 2 * NG * (i + 1), "wr_mask", 16)
                read_stack("q", i + 1, Q_RUNS)
                read_stack("k", i + 1, k_runs)
            if on(i + 2):
                wait(sp, "V", i + 2)
                sp.dma_start(xT[:, :, :], ap["xT"][bass.ds(i + 2, 1)].rearrange("b (k p) n -> p (b k) n", p=P)
                             ).then_inc(sem("ld_xT"), 16)
            experts_out(i, mode, 0)
            if mode == "scale":
                wait(sp, "wmax0", NE)
                experts_in(i + 1, "halve", 0)
            elif not (isinstance(i, int) and i in (6, B - 1)):
                experts_in(i + 1, mode, 0)
            if on(i):
                write_parts("ck", i)
            if on(i - 2):
                wait(sp, "x2", i - 1)
                sp.dma_start(YS[0:T, :].rearrange("(b t p) d -> b t p d", t=QT, p=P)[bass.ds(i - 2, 1)]
                             .rearrange("b t p d -> p (b t) d"), x2s[:, :, :]).then_inc(sem("wr_x2"), 16)
                sp.dma_start(X2R[:, bass.ds(QT * (i - 2), QT), 0:D], x2s[:, :, :]).then_inc(sem("wr_x2"), 16)
            experts_out(i, mode, 1)
            fill_rows(i)
            if isinstance(i, int) and i < 0:
                sp.wait_ge(sem("mask_parts"), 1)
                sp.dma_start(dmask, maskp[:, :, :]).then_inc(sem("wr_mask"), 16)
                sp.wait_ge(sem("wr_mask"), 16)

        load_expert(0, 0)
        iterations(step, sp)

        sp.wait_ge(sem("wr_x2"), 32 * B)
        sp.wait_ge(sem("wr_fill"), 16 * (len(FILL_STEPS) + 1))
        for k in range(2):
            sp.wait_ge(sem(f"wr_w{k}"), 16 * NE)

    @block.tensor
    def _(pe):
        pe.wait_ge(sem("ld_w"), 48)

        def put_cols(name, w, rhs, n):
            out = BK[BANK[name]][:, :].rearrange("p (k n) -> p k n", k=KT)
            for m in range(KT):
                for k in range(KT):
                    mm = pe.matmul(out[:, m, 0:n], w[:, k, m * P:(m + 1) * P], rhs[:, k, :],
                                   start=(k == 0), stop=(k == KT - 1))
            mm.then_inc(sem(name), 1)

        def put_rows(name, lhs, w, tiles, m):
            out = BK[BANK[name]][:, :].rearrange("p (t n) -> p t n", n=D)
            for t in range(tiles):
                for k in range(KT):
                    mm = pe.matmul(out[0:m, t, :], lhs[:, k, t * P:t * P + m], w[:, k, :],
                                   start=(k == 0), stop=(k == KT - 1))
            mm.then_inc(sem(name), 1)

        def put_turned(name, src):
            out = BK[BANK[name]][:, :].rearrange("p (k n) -> p k n", k=KT)
            for k in range(KT):
                for t in range(QT):
                    mm = pe.transpose(out[:, k, t * P:(t + 1) * P], src[:, t, k * P:(k + 1) * P], ident[:, :])
            mm.then_inc(sem(name), 1)

        def item(name, b, i):
            if not on(b):
                return
            bank_free(pe, name, i)
            if name == "Q":
                wait(pe, "ld_xT", 16 * (b + 1))
                put_cols(name, wq, xT, L)
            elif name == "K":
                put_cols(name, wk, xT, L)
            elif name == "V":
                put_rows(name, xT, wv, QT, P)
            elif name == "T1":
                if isinstance(i, int) and i <= 1:
                    wait(pe, "ld_const", 16)
                    wait(pe, "ld_w2", 80)
                wait(pe, "x1", b + 1)
                put_turned(name, x1s)
            elif name == "Qc":
                wait(pe, "read_T1", b + 1)
                put_cols(name, cq, x1T, L)
            elif name == "Kc":
                if isinstance(i, int) and i == 0:
                    wait(pe, "ld_w2", 80)
                wait(pe, "ld_cT", 16 * (b + 1))
                put_cols(name, ck, cT, LC)
            elif name == "Vc":
                put_rows(name, cT, cv, 1, LC)
            elif name in ("AOT", "AOTc"):
                wait(pe, "norm" if name == "AOT" else "normc", NG * (b + 1))
                if isinstance(i, int) and i <= 0:
                    wait(pe, "ld_const", 16)
                put_turned(name, ao)
            elif name in ("O", "Oc"):
                wait(pe, "read_AOT" if name == "O" else "read_AOTc", b + 1)
                put_rows(name, aoT, wo if name == "O" else co, QT, P)
            elif name == "T2":
                wait(pe, "x2", b + 1)
                put_turned(name, x2s)
            elif name == "R":
                if isinstance(i, int):
                    wait(pe, "ld_gate", 16)
                wait(pe, "read_T2", b + 1)
                for t in range(QT):
                    for k in range(KT):
                        mm = pe.matmul(BK[1][:, t * NE:(t + 1) * NE], x2T[:, k, t * P:(t + 1) * P],
                                       gate[:, k, :], start=(k == 0), stop=(k == KT - 1))
                mm.then_inc(sem(name), 1)

        def scores(u, half, i):
            if u < NG:
                b, g = i, u
                if not on(b):
                    return
                wait(pe, "max", 2 * NG * b + 2 * g + half)
                if g == 0 and half == 0:
                    wait(pe, "maxc", NG * (i - 1))
                    if isinstance(i, int) and i == 0:
                        wait(pe, "aux_set", 64)
                    wait(pe, "st_q", 16 * N_Q * (b + 1))
                    wait(pe, "st_k", 16 * N_K * (b + 1))
                for j in range(2):
                    h = GH * g + 2 * half + j
                    for t in range(QT):
                        mm = pe.matmul(SA[:, j, t * L:(t + 1) * L],
                                       stack["q"][0:PROD + PARTS, h, t * P:(t + 1) * P],
                                       stack["k"][0:PROD + PARTS, h, :], start=True, stop=True)
                mm.then_inc(sem("S"), 1)
            elif half == 0:
                b, g = i - 1, u - NG
                if not on(b):
                    return
                wait(pe, "maxc", NG * b + g)
                if g == 0:
                    wait(pe, "max", 2 * NG * (i + 1) if on(i) else 2 * NG * B)
                    wait(pe, "st_cq", 16 * N_Q * (b + 1))
                    wait(pe, "st_ck", 16 * (N_K + 1) * (b + 1))
                for j in range(GH):
                    h = GH * g + j
                    for t in range(QT):
                        at = (2 * (j % 2) + t) * LC
                        mm = pe.matmul(SA[:, j // 2, at:at + LC],
                                       stack["cq"][0:PROD + PARTS, h, t * P:(t + 1) * P],
                                       stack["ck"][0:PROD + PARTS, h, :], start=True, stop=True)
                mm.then_inc(sem("Sc"), 1)

        def maxima(u, i):
            mine, b, g = group(u, i, 1)
            if not on(b):
                return
            c = "" if mine else "c"
            wait(pe, f"mparts{c}", NG * b + g + 1)
            last(pe, u, i, 2, "mcopy")
            for t in range(QT):
                mm = pe.transpose(MT[0:AUX, t * P:(t + 1) * P], MTp[:, t, 0:AUX], identb[:, :])
            mm.then_inc(sem(f"MT{c}"), 1)

        def keyed(u, half, i):
            mine, b, g = group(u, i, 1)
            if not on(b) or (not mine and half == 1):
                return
            if half == 0:
                last(pe, u, i, 2, "E", 2)
            if mine:
                if half == 0:
                    wait(pe, "aux", NG * b + g + 1)
                else:
                    wait(pe, "E", 2 * (NG * b + g) + 1)
                for j in range(2):
                    h = GH * g + 2 * half + j
                    for k in range(QT):
                        mm = pe.matmul(SB[:, j, k * L:(k + 1) * L],
                                       stack["k"][:, h, k * P:(k + 1) * P],
                                       stack["q"][:, h, :], start=True, stop=True)
                mm.then_inc(sem("ST"), 1)
            else:
                wait(pe, "auxc", NG * b + g + 1)
                for j in range(GH):
                    h = GH * g + j
                    mm = pe.matmul(SB[0:LC, j // 2, (j % 2) * L:(j % 2 + 1) * L],
                                   stack["ck"][:, h, :], stack["cq"][:, h, :], start=True, stop=True)
                mm.then_inc(sem("STc"), 1)

        def weigh(u, i):
            mine, b, g = group(u, i, 2)
            if not on(b):
                return
            c = "" if mine else "c"
            last(pe, u, i, 3, "norm")
            wait(pe, f"E{c}", (2 if mine else 1) * (NG * b + g + 1))
            wait(pe, f"read_V{c}", b + 1)
            slot = u % 2
            for k in range(QT if mine else 1):
                for j in range(GH):
                    h = GH * g + j
                    if mine:
                        mm = pe.matmul(AV[32 * j:32 * j + 32, 0:L], V[:, k, h, :], PT[:, slot, j, k, :],
                                       start=(k == 0), stop=(k == QT - 1))
                    else:
                        mm = pe.matmul(AV[32 * j:32 * j + 32, 0:L], CV[0:LC, h, :],
                                       PT[0:LC, slot, j, 0, :], start=True, stop=True)
            mm.then_inc(sem(f"AV{c}"), 1)

        def turn_weighed(u, i):
            mine, b, g = group(u, i, 3)
            if not on(b):
                return
            c = "" if mine else "c"
            wait(pe, f"avs{c}", NG * b + g + 1)
            for t in range(QT):
                mm = pe.transpose(AV[:, t * P:(t + 1) * P], avs[:, t * P:(t + 1) * P], ident[:, :])
            mm.then_inc(sem(f"AVT{c}"), 1)

        def gap(u, half, i):
            if (u, half) in GAPS:
                name, off = GAPS[u, half]
                item(name, i + off, i)

        def step(i, mode):
            for u in range(2 * NG):
                if u < NG:
                    scores(u, 0, i)
                    turn_weighed(u, i)
                    maxima(u, i)
                else:
                    maxima(u, i)
                    turn_weighed(u, i)
                    scores(u, 0, i)
                gap(u, 0, i)
                scores(u, 1, i)
                keyed(u, 0, i)
                weigh(u, i)
                gap(u, 1, i)
                keyed(u, 1, i)

        iterations(step, pe)

    @block.vector
    def _(dve):
        chain = Chain(dve, sem("dve_chain"))

        dve.wait_ge(sem("ld_cols"), 64)
        for n in (1, 3):
            dve.tensor_scalar(cols[:, n, :], cols[:, n, :], SQ, None, ALU.mult).then_inc(sem("cols"), 1)
        dve.memset(MTp[:, :, :], 1.0)
        dve.wait_ge(sem("ld_const"), 16)
        dve.tensor_copy(identb[:, :], ident[:, :]).then_inc(sem("identb"), 1)
        dve.wait_ge(sem("ld_mask"), 16)
        chain(dve.tensor_scalar(maskr[:, 0, :], maskt[:, :], -1e9, None, ALU.mult))
        chain(dve.tensor_copy(maskp[:, 0, :], maskr[:, 0, :]))
        chain(dve.tensor_tensor(maskr[:, 1, :], maskr[:, 0, :], maskp[:, 0, :], ALU.subtract))
        chain(dve.tensor_copy(maskp[:, 1, :], maskr[:, 1, :]))
        dve.tensor_tensor(maskp[:, 2, :], maskr[:, 1, :], maskp[:, 1, :], ALU.subtract).then_inc(sem("mask_parts"), 1)

        def top(u, half, i):
            mine, b, g = group(u, i, 0)
            if not on(b) or (not mine and half == 1):
                return
            if mine:
                wait(dve, "S", 2 * (NG * b + g) + half + 1)
                dve.tensor_reduce(mneg[:, :, 2 * half:2 * half + 2].rearrange("p t j -> p j t"),
                                  SA[:, :, :].rearrange("p j (t n) -> p j t n", n=L),
                                  AX.X, ALU.max, negate=True).then_inc(sem("max"), 1)
            else:
                wait(dve, "Sc", NG * b + g + 1)
                dve.tensor_reduce(mneg[:, :, :].rearrange("p t j -> p j t"),
                                  SA[:, :, 0:4 * LC].rearrange("p a (c n) -> p a c n", n=LC),
                                  AX.X, ALU.max, negate=True).then_inc(sem("maxc"), 1)

        def spread_and_divide(u, i):
            mine, b, g = group(u, i, 1)
            mine3, b3, g3 = group(u, i, 3)
            c, q = ("", "q") if mine else ("c", "cq")
            c3 = "" if mine3 else "c"
            if on(b):
                wait(dve, f"MT{c}", NG * b + g + 1)
                dve.tensor_copy(mts[0:AUX, :], MT[0:AUX, 0:L]).then_inc(sem(f"mcopy{c}"), 1)
            turned = AV[:, 0:QT * P].rearrange("p (t j c) -> p t j c", t=QT, c=2 * HD)
            if on(b3):
                wait(dve, f"AVT{c3}", NG * b3 + g3 + 1)
                chain.put(dve.reciprocal(rc[:, :, :], turned[:, :, :, HD]))
            if on(b):
                wait(dve, f"mcopy{c}", NG * b + g + 1)
                dve.tensor_copy(stack[q][PROD:PROD + AUX, GH * g:GH * g + GH, :],
                                mts[0:AUX, :].unsqueeze(1).to_broadcast([AUX, GH, L])
                                ).then_inc(sem(f"aux{c}"), 1)
            if on(b3):
                chain.wait()
                if g3 == 0:
                    wait(dve, "AOT", i if mine3 else i + 1) if on(i) else wait(dve, "AOT", B)
                    wait(dve, "AOTc", b3 - 1 if mine3 else b3)
                dve.tensor_tensor(ao[:, :, GH * HD * g3:GH * HD * (g3 + 1)].rearrange("p t (j c) -> p t j c", c=HD),
                                  turned[:, :, :, 0:HD],
                                  rc[:, :, :].unsqueeze(3).to_broadcast([P, QT, GH, HD]), ALU.mult
                                  ).then_inc(sem(f"norm{c3}"), 1)

        def split_maxima(u, i):
            mine, b, g = group(u, i, 0)
            c = "" if mine else "c"
            p0, p1, p2 = (MTp[:, :, 3 + GH * a:3 + GH * (a + 1)] for a in range(PARTS))
            if on(b):
                wait(dve, f"max{c}", (2 if mine else 1) * (NG * b + g + 1))
                chain.put(dve.tensor_copy(p0, mneg[:, :, :]))
            if on(b):
                chain.wait()
                chain.put(dve.tensor_tensor(mr[:, :, :], mneg[:, :, :], p0, ALU.subtract))
            gap(u, 0, i)
            if on(b):
                chain.wait()
                chain(dve.tensor_copy(p1, mr[:, :, :]))
                dve.tensor_tensor(p2, mr[:, :, :], p1, ALU.subtract).then_inc(sem(f"mparts{c}"), 1)

        def item(name, b, i):
            if not on(b) or name not in ("V", "Vc", "O", "Oc", "R"):
                return
            wait(dve, name, b + 1)
            if name == "V":
                wait(dve, "ld_rows", 64) if isinstance(i, int) and i < 0 else None
                wait(dve, "ones", 3) if isinstance(i, int) and i < 0 else None
                wait(dve, "AV", NG * b)
                dve.tensor_tensor(V[:, :, :, 0:HD],
                                  BK[1][:, :].rearrange("p (t h d) -> p t h d", t=QT, d=HD),
                                  rows_b[:, 0, :].rearrange("p (h d) -> p h d", d=HD).unsqueeze(1)
                                  .to_broadcast([P, QT, H, HD]), ALU.add).then_inc(sem("read_V"), 1)
            elif name == "Vc":
                wait(dve, "AVc", NG * b)
                dve.tensor_tensor(CV[0:LC, :, 0:HD], BK[1][0:LC, 0:D].rearrange("p (h d) -> p h d", d=HD),
                                  rows_b[0:LC, 2, :].rearrange("p (h d) -> p h d", d=HD), ALU.add
                                  ).then_inc(sem("read_Vc"), 1)
            elif name == "R":
                dve.tensor_copy(LG[:, bass.ds(QT * b, QT), :].rearrange("p t n -> p (t n)"),
                                BK[1][:, 0:QT * NE]).then_inc(sem("read_R"), 1)
            else:
                c = name[1:]
                wait(dve, "xbo" if name == "O" else "x1bo", b + 1)
                dve.tensor_tensor(r1[:, :, :], BK[1][:, :].rearrange("p (t n) -> p t n", n=D),
                                  (xbo if name == "O" else x1bo)[:, :, :], ALU.add
                                  ).then_inc(sem(f"read_{name}"), 1)
                wait(dve, f"read_{name}", b + 1)
                for t in range(QT):
                    ins = dve.bn_stats(stats[:, t, :], r1[:, t, :])
                    ins.then_inc(sem(f"stats{c}"), 1)
                wait_apart(dve, f"stats{c}", QT * (b + 1), "identb", 1)
                for t in range(QT):
                    dve.bn_aggr(mv[:, t, :], stats[:, t, :]).then_inc(sem(f"mv{c}"), 1)

        def gap(u, half, i):
            if (u, half) in GAPS:
                name, off = GAPS[u, half]
                item(name, i + off, i)

        def weights(u, i, mode):
            if mode != "max":
                return
            k, c = divmod(u, NG)
            wait(dve, f"ld_wst{k}", 16 * (i + 2))
            ins = dve.tensor_reduce(wmx[:, k, c, bass.ds(i + 1, 1)], wst[k][:, c * QW:(c + 1) * QW], AX.X, ALU.max,
                                    apply_absolute_value=True)
            if c == NG - 1:
                ins.then_inc(sem(f"wmax{k}"), 1)

        def halves(u, i, mode):
            if mode != "halve":
                return
            k, c = divmod(u, NG)
            wait(dve, f"whi{k}", NG * (i - 8) + c + 1)
            ins = dve.scalar_tensor_tensor(half_of(k, 1, c), quarter(k, c), SC[:, k:k + 1], half_of(k, 0, c),
                                           ALU.mult, ALU.subtract)
            if c == NG - 1:
                ins.then_inc(sem(f"wlo{k}"), 1)

        def greatest():
            dve.wait_ge(sem("ld_b1"), 16)
            for k in range(2):
                dve.wait_ge(sem(f"wmax{k}"), NE)
            dve.tensor_reduce(wm[:, 0:2], wmx[:, :, :, :].rearrange("p k c e -> p k (c e)"), AX.X, ALU.max)
            dve.tensor_reduce(wm[:, 2:3], b1t[:, :, :].rearrange("p e f -> p (e f)"), AX.X, ALU.max,
                              apply_absolute_value=True).then_inc(sem("wm"), 1)

        def scales():
            dve.wait_ge(sem("wg"), 1)
            chain(dve.tensor_copy(wp[:, 0:2], wg[:, 0:2]))
            chain(dve.tensor_scalar(wp[:, 2:3], wg[:, 0:1], float(D), wg[:, 2:3], ALU.mult, ALU.add))
            chain(dve.tensor_scalar(wp[:, 0:3], wp[:, 0:3], 2.0 ** -100, 2.0 ** 100, ALU.max, ALU.min))
            bits = wp[:, 0:3].bitcast(I32)
            chain(dve.tensor_scalar(bits, bits, 0x7F800000, None, ALU.bitwise_and))
            chain(dve.reciprocal(wp[:, 3:6], wp[:, 0:3]))
            chain(dve.tensor_scalar(SC[:, 0:2], wp[:, 3:5], 2.0 ** 13, None, ALU.mult))
            chain(dve.tensor_scalar(SC[:, 2:3], wp[:, 5:6], 2.0 ** 14, None, ALU.mult))
            chain(dve.tensor_scalar(SC[:, 3:4], SC[:, 2:3], wp[:, 0:1], 2.0 ** -13, ALU.mult, ALU.mult))
            chain(dve.tensor_scalar(SC[:, 4:5], wp[:, 1:2], wp[:, 2:3], 2.0 ** -27, ALU.mult, ALU.mult))
            dve.tensor_scalar(b1c[:, :, :], b1t[:, :, :], SC[:, 2:3], None, ALU.mult).then_inc(sem("scales"), 1)

        def step(i, mode):
            for u in range(2 * NG):
                if mode == "scale" and u == 0:
                    greatest()
                if mode == "scale" and u == 3:
                    scales()
                if u < NG:
                    top(u, 0, i)
                    spread_and_divide(u, i)
                else:
                    spread_and_divide(u, i)
                    top(u, 0, i)
                top(u, 1, i)
                split_maxima(u, i)
                weights(u, i, mode)
                if u:
                    halves(u - 1, i, mode)
                gap(u, 1, i)
                if u == 2 * NG - 1:
                    halves(u, i, mode)

        iterations(step, dve, chain, 8 * 3 + 8)

    @block.scalar
    def _(act):
        def item(name, b, i):
            if not on(b) or name in ("V", "Vc", "O", "Oc", "R"):
                return
            wait(act, name, b + 1)
            bank = BK[BANK[name]][:, :].rearrange("p (k n) -> p k n", k=KT)
            if name in ("Q", "K", "Qc", "Kc"):
                n = dict(Q="q", K="k", Qc="cq", Kc="ck")[name]
                c = names.index(n)
                scale = SQ if name[0] == "K" else 1.0
                if isinstance(i, int) and i <= 1:
                    wait(act, "cols", 2)
                wait(act, f"parts_{n}", b)
                for k in range(KT):
                    ins = act.activation(full[n][:, k, :], bank[:, k, 0:width[n]], ACT.Identity,
                                         bias=cols[:, c, k:k + 1], scale=scale)
                    ins.then_inc(sem(f"read_{name}"), 1) if k == KT - 1 else ins.then_inc(sem(f"half_{name}"), 1)
            else:
                dst = dict(T1=x1T, T2=x2T, AOT=aoT, AOTc=aoT)[name]
                act.activation(dst[:, :, :], bank, ACT.Copy).then_inc(sem(f"read_{name}"), 1)

        def gap(u, half, i):
            if (u, half) in GAPS:
                name, off = GAPS[u, half]
                item(name, i + off, i)

        def late(c, b):
            if not on(b):
                return
            wait(act, f"rstd{c}", b + 1)
            if c:
                wait(act, "wr_x2", 32 * b)
            else:
                wait(act, "x1bo", b)
            for t in range(QT):
                ins = act.activation((x2s if c else x1s)[:, t, :], r1[:, t, :], ACT.Identity,
                                     bias=shift[:, t:t + 1], scale=rstd[:, t:t + 1])
            ins.then_inc(sem("x2" if c else "x1"), 1)

        def first_part(u, half, i):
            name, off = GAPS.get((u, half), ("", 0))
            b = i + off
            if name in ("Q", "K", "Qc", "Kc") and on(b):
                n = dict(Q="q", K="k", Qc="cq", Kc="ck")[name]
                wait(act, f"read_{name}", b + 1)
                wait(act, f"half_{name}", b + 1)
                wait(act, f"wr_{n}", 16 * b)
                act.activation(part[n][:, :, 0, :], full[n][:, :, :], ACT.Copy).then_inc(sem(f"part0_{n}"), 1)

        def exps(u, half, i):
            mine, b, g = group(u, i, 1)
            if not on(b) or (not mine and half == 1):
                return
            slot = (u - 1) % 2
            if half == 0:
                last(act, u, i, 3, "AV")
                if isinstance(i, int) and i == 0:
                    wait(act, "aux_set", 64)
            if mine:
                wait(act, "ST", 2 * (NG * b + g) + half + 1)
                act.activation(PT[:, slot, 2 * half:2 * half + 2, :, :].rearrange("p j k n -> p (j k n)"),
                               SB[:, :, :].rearrange("p j n -> p (j n)"), ACT.Exp).then_inc(sem("E"), 1)
            else:
                wait(act, "STc", NG * b + g + 1)
                act.activation(PT[0:LC, slot, :, 0, :],
                               SB[0:LC, :, :].rearrange("p a (c n) -> p (a c) n", n=L), ACT.Exp
                               ).then_inc(sem("Ec"), 1)

        def store_weighed(u, i):
            mine, b, g = group(u, i, 2)
            if not on(b):
                return
            c = "" if mine else "c"
            wait(act, f"AV{c}", NG * b + g + 1)
            act.activation(avs[:, :], AV[:, 0:L], ACT.Copy).then_inc(sem(f"avs{c}"), 1)

        def weights(u, i, mode):
            if mode != "halve":
                return
            k, c = divmod(u, NG)
            act.wait_ge(sem("scales"), 1)
            if c == 0:
                wait(act, f"ld_wst{k}", 16 * (i + 1))
                wait(act, f"wr_w{k}", 16 * (i - 8))
            act.activation(half_of(k, 0, c), quarter(k, c), ACT.Copy, scale=SC[:, k:k + 1]
                           ).then_inc(sem(f"whi{k}"), 1)

        def step(i, mode):
            for u in range(2 * NG):
                gap(u, 0, i)
                if u == 0:
                    late("", i - 1)
                if u == 5:
                    late("c", i - 2)
                exps(u, 0, i)
                first_part(u, 0, i)
                store_weighed(u, i)
                exps(u, 1, i)
                gap(u, 1, i)
                first_part(u, 1, i)
                weights(u, i, mode)

        iterations(step, act)

    @block.gpsimd
    def _(pool):
        chain = Chain(pool, sem("pool_chain"), nc, (sem("ones"), 3))
        pool.memset(V[:, :, :, :], 1.0).then_inc(sem("ones"), 1)
        pool.memset(CV[:, :, :], 1.0).then_inc(sem("ones"), 1)
        pool.memset(mhalf[:, :], -0.5).then_inc(sem("ones"), 1)
        pool.memset(minus[:, QT:QT + 1], 0.0).then_inc(sem("minus"), 1)
        pool.memset(minus[:, 0:QT], -1.0).then_inc(sem("minus"), 1)
        pool.wait_ge(sem("ones"), 3)
        pool.wait_ge(sem("minus"), 2)
        pool.wait_ge(sem("ld_rows"), 64)

        def split(n, b):
            if not on(b):
                return
            wait(pool, f"part0_{n}", b + 1)
            chain(pool.tensor_tensor(rest[n][:, :, :], full[n][:, :, :], part[n][:, :, 0, :], ALU.subtract))
            chain(pool.tensor_tensor(part[n][:, :, 1, :], rest[n][:, :, :],
                                     minus[:, 2:3].unsqueeze(1).to_broadcast([P, KT, width[n]]), ALU.add))
            pool.tensor_tensor(part[n][:, :, 2, :], rest[n][:, :, :], part[n][:, :, 1, :], ALU.subtract
                               ).then_inc(sem(f"parts_{n}"), 1)

        def deviations(c, b):
            if not on(b):
                return
            wait_apart(pool, f"mv{c}", QT * (b + 1), "ones", 3)
            chain(pool.tensor_scalar(ve[:, :], mv[:, :, 1], EPS, None, ALU.add))
            ins = pool.tensor_tensor(rstd[:, :], ve[:, :], mhalf[:, 0:QT], ALU.pow)
            chain(ins)
            chain(pool.tensor_tensor(shift[:, :], mv[:, :, 0], rstd[:, :], ALU.mult))
            pool.tensor_tensor(shift[:, :], shift[:, :], minus[:, 0:QT], ALU.mult).then_inc(sem(f"rstd{c}"), 1)

        def step(i, mode):
            if mode == "scale":
                pool.wait_ge(sem("wm"), 1)
                pool.partition_all_reduce(wg[:, :], wm[:, :], P, bass.bass_isa.ReduceOp.max
                                          ).then_inc(sem("wg"), 1)
            split("q", i + 1)
            split("cq", i - 1)
            deviations("c", i - 2)
            if on(i - 1):
                wait(pool, "x1", i)
                wait(pool, "read_Oc", i - 1)
                pool.tensor_tensor(x1bo[:, :, :], x1s[:, :, :],
                                   rows_b[:, 3, :].unsqueeze(1).to_broadcast([P, QT, D]), ALU.add
                                   ).then_inc(sem("x1bo"), 1)
            split("k", i + 1)
            split("ck", i)
            if on(i):
                wait(pool, "ld_x", 16 * (i + 1))
                wait(pool, "read_O", i)
                pool.tensor_tensor(xbo[:, :, :], xrow[:, :, :],
                                   rows_b[:, 1, :].unsqueeze(1).to_broadcast([P, QT, D]), ALU.add
                                   ).then_inc(sem("xbo"), 1)
            deviations("", i)

        iterations(step, pool, chain, 4 * 2 + 6)


def experts(nc, ctx, ap, outer, sem):
    ident, identb, mhalf, LG, X2R, SC, b1c, dW, XS, YS = (outer[n] for n in (
        "ident", "identb", "mhalf", "LG", "X2R", "SC", "b1c", "dW", "XS", "YS"))

    def sb(name, shape, dt=F32):
        return ctx.enter_context(nc.sbuf_tensor(name, shape, dt))

    def ps(name, shape, dt=F32):
        return ctx.enter_context(nc.psum_tensor(name, shape, dt))

    W = sb("W", [P, NE, 2, 2, WC], F16)
    b2r = sb("b2r", [P, NE, D])
    tri = sb("tri", [P, P])
    ones = sb("ones2", [P, P])
    ids = sb("ids", [P, NT])
    desc = sb("desc", [P, NE])
    jrow = sb("jrow", [P, NBLK + 1])
    big = [P, NT, NE]
    ex = sb("ex", big)
    pr = sb("pr", big)
    eq = sb("eq", big)
    oh = [sb(f"oh{k}", big) for k in range(2)]
    both = sb("both", big)
    at = sb("at", big)
    cum = sb("cum", [P, NE, NT])
    small = sb("small", [P, 6, NT])
    cnt = sb("cnt", [P, 6, NE])
    cnti = sb("cnti", [P, 2, NE], I32)
    cmp = sb("cmp", [P, NBLK + 1, NE])
    BEf = sb("BEf", [P, NBLK + 1])
    BEi = sb("BEi", [P, NBLK + 1], I32)
    PKf = sb("PKf", [P, NBLK])
    PKi = sb("PKi", [P, NBLK], I32)
    pos = sb("pos", [P, 2, NT])
    posu = sb("posu", [P, 2, NT], U32)
    XB = [sb(f"XB{k}", [P, ROW]) for k in range(2)]
    xhi = [sb(f"xhi{k}", [P, KT, P], F16) for k in range(2)]
    xlo = [sb(f"xlo{k}", [P, KT, P], F16) for k in range(2)]
    hhi = [sb(f"hhi{k}", [P, FT, P], F16) for k in range(3)]
    hlo = [sb(f"hlo{k}", [P, FT, P], F16) for k in range(3)]
    wsel = sb("wsel", [P, 4])
    wv = [sb(f"wv{k}", [P, 1]) for k in range(6)]
    tok = [sb(f"tok{k}", [P, 1], U32) for k in range(6)]
    yl = sb("yl", [P, D])
    yb = sb("yb", [P, D])
    ysc = [sb(f"ysc{k}", [P, D]) for k in range(2)]
    stats = sb("stats2", [P, 4, 6])
    mv = [sb(f"mv2_{k}", [P, 4, 2]) for k in range(2)]
    ve = sb("ve2", [P, 4])
    rstd = [sb(f"rstd2_{k}", [P, 4]) for k in range(2)]
    shift = [sb(f"shift2_{k}", [P, 4]) for k in range(2)]

    HB = [ps(f"HB{k}", [P, 2, 512]) for k in range(2)]
    XTp = ps("XTp", [P, 512])
    YP0 = ps("YP0", [P, 512])
    R0 = ps("R0", [P, 512])
    R1 = ps("R1", [P, 512])
    YP = [YP0, R0]
    NS = NT // 4
    ROUND, HEAD, LAG = 6, 6, 3
    ROUNDS = (NBLK - HEAD - 2) // ROUND

    block = ctx.enter_context(nc.Block())

    def wait(eng, name, val):
        if not isinstance(val, int) or val > 0:
            eng.wait_ge(sem(name), val)

    def wait_apart(eng, name, val, held, count):
        if not isinstance(val, int) or val > 0:
            apart(nc, eng, sem(name), val, (sem(held), count))

    def blocks(step, eng, chain=None, per=0, start=None):
        for j in range(HEAD):
            step(j, j)
        n = chain.n if chain else 0
        with eng.Fori(0, ROUNDS) as m:
            if chain:
                chain.n, chain.count = n + ROUND * per * m, 0
            if start:
                start(m)
            for r in range(ROUND):
                step(ROUND * m + (HEAD + r), HEAD + r)
            assert not chain or chain.count == ROUND * per, chain.count
        if chain:
            chain.n = n + per * ROUND * ROUNDS
        for j in range(HEAD + ROUND * ROUNDS, NBLK + LAG):
            step(j, j)

    def packed(eng, m, found):
        word = eng.value_load(PKi[0:1, bass.ds(m, 1)], min_val=0, max_val=(1 << 24) - 1)
        for r in range(ROUND + 2):
            found[HEAD - 2 + r] = (word >> (3 * r)) & (NE - 1)

    @block.sync
    def _(sp):
        for dst, name in ((ids[:, :], "ids"), (tri[:, :], "tri"), (desc[:, :], "desc"), (jrow[:, :], "jrow")):
            sp.dma_start(dst, ap[name]).then_inc(sem("ld_route"), 16)
        sp.dma_start(b2r[:, :, :].rearrange("p e d -> p (e d)"),
                     ap["b2"].rearrange("e d -> (e d)").partition_broadcast(P)).then_inc(sem("ld_b2"), 16)
        sp.dma_start(W[:, 0].rearrange("p a c n -> p (a c n)"), dW[0].rearrange("p a c n -> p (a c n)")
                     ).then_inc(sem("ld_W"), 16)

        def load_rows(j, q):
            sp.dma_start(XB[q][:, :], XS.rearrange("(j p) c -> j p c", p=P)[bass.ds(j, 1)]
                         .rearrange("j p c -> p (j c)")).then_inc(sem("ld_XB"), 16)

        sp.wait_ge(sem("scatter"), 16 * 2 * NT)
        load_rows(0, 0)
        for e in range(1, NE):
            sp.wait_ge(sem("ld_W"), 16 * e)
            sp.dma_start(W[:, e].rearrange("p a c n -> p (a c n)"), dW[e].rearrange("p a c n -> p (a c n)")
                         ).then_inc(sem("ld_W"), 16)
            if e == 1:
                sp.wait_ge(sem("ld_XB"), 16)
                load_rows(1, 1)

        def step(j, n):
            if isinstance(j, int) and j + 2 >= NBLK:
                return
            wait(sp, "XT", j + 1)
            wait(sp, "wv", j + 1)
            wait(sp, "tok", j + 1)
            wait(sp, "ld_XB", 16 * (j + 2))
            load_rows(j + 2, n % 2)

        blocks(step, sp)
        sp.wait_ge(sem("add"), 16 * NBLK)
        rows = YS[0:T, :].rearrange("(t p) d -> p t d", p=P)
        for s in range(NS):
            sp.dma_start(X2R[:, 4 * s:4 * s + 4, 0:D], rows[:, 4 * s:4 * s + 4, :]).then_inc(sem(f"ld_Y{s}"), 16)
        for s in range(NS):
            sp.wait_ge(sem("fin"), s + 1)
            sp.dma_start(ap["out"].rearrange("(t p) d -> p t d", p=P)[:, 4 * s:4 * s + 4, :],
                         X2R[:, 4 * s:4 * s + 4, 0:D]).then_inc(sem("wr_out"), 16)
        sp.wait_ge(sem("wr_out"), 16 * NS)

    @block.tensor
    def _(pe):
        pe.wait_ge(sem("ld_route"), 64)
        pe.wait_ge(sem("ones_r"), 1)
        pe.wait_ge(sem("both"), 1)
        flat = both[:, :, :].rearrange("p t e -> p (t e)")
        pe.matmul(R0[:, 0:NT * NE], tri[:, :], flat, start=True, stop=True)
        pe.matmul(R1[:, 0:NT * NE], ones[:, :], flat, start=True, stop=True).then_inc(sem("counts"), 1)

        def turn(j, n):
            wait(pe, "ld_XB", 16 * (j + 1))
            wait(pe, "xlo", j)
            for k in range(KT):
                mm = pe.transpose(XTp[:, k * P:(k + 1) * P], XB[n % 2][:, k * P:(k + 1) * P], ident[:, :])
            mm.then_inc(sem("XT"), 1)

        found, peeled = {}, {}

        def expert(j, n):
            if not isinstance(j, int):
                return found[n]
            if j not in peeled:
                peeled[j] = pe.value_load(BEi[0:1, bass.ds(j, 1)], min_val=0, max_val=NE - 1)
            return peeled[j]

        def first(n, e, f):
            out = HB[n % 2][:, f // 4, (f % 4) * P:(f % 4 + 1) * P]
            for k in range(KT):
                for half, x in ((0, xhi), (0, xlo), (1, xhi)):
                    w = W[:, bass.ds(e, 1), 0, half, k * F + f * P:k * F + (f + 1) * P]
                    mm = pe.matmul(out, w.rearrange("p e n -> p (e n)"), x[n % 2][:, k, :],
                                   start=(k == 0 and half == 0 and x is xhi), stop=(k == KT - 1 and half == 1))
            if f % 4 == 3:
                mm.then_inc(sem("HB"), 1)

        def second(n, e, f):
            w = W[:, bass.ds(e, 1), 1].rearrange("p e c n -> p (e c n)")[:, 2 * D * f:2 * D * (f + 1)]
            if f > 0:
                pe.matmul(YP[n % 2][:, 0:D], hlo[n % 3][:, f, :], w[:, 0:D], start=False, stop=False)
            mm = pe.matmul(YP[n % 2][:, :], hhi[n % 3][:, f, :], w, start=(f == 0), stop=(f == FT - 1))
            if f == 0:
                pe.matmul(YP[n % 2][:, 0:D], hlo[n % 3][:, f, :], w[:, 0:D], start=False, stop=False)
            if f == FT - 1:
                mm.then_inc(sem("YP"), 1)

        pe.wait_ge(sem("table"), 1)

        def step(j, n):
            fixed = isinstance(j, int)
            now, before = not (fixed and j >= NBLK), not (fixed and not 2 <= j < NBLK + 2)
            if fixed and j == 0:
                turn(0, 0)
            e = expert(j, n) if now else None
            e2 = expert(j - 2, n - 2) if before else None
            if now:
                pe.wait_ge(sem("ld_W"), 16 * e + 16)
                wait(pe, "xlo", j + 1)
            if before:
                wait(pe, "hlo", 2 * (j - 1))
                if not (fixed and j < 4):
                    wait(pe, "yb", j - 3)
            for f in range(FT):
                if now:
                    first(n, e, f)
                if f == 3 and not (fixed and j >= NBLK - 1):
                    turn(j + 1, n + 1)
                if before:
                    second(n - 2, e2, f)

        blocks(step, pe, start=lambda m: packed(pe, m, found))

    @block.scalar
    def _(act):
        act.wait_ge(sem("centred"), 1)
        act.activation(ex[:, :, :], eq[:, :, :], ACT.Exp).then_inc(sem("ex"), 1)

        def xhalf(j, n):
            wait(act, "XT", j + 1)
            if not (isinstance(j, int) and j < 2):
                wait(act, "HB", 2 * (j - 1))
            act.activation(xhi[n % 2][:, :, :], XTp[:, 0:D].rearrange("p (k n) -> p k n", k=KT), ACT.Copy
                           ).then_inc(sem("xhi"), 1)

        def hidden(j, n):
            if not (isinstance(j, int) and j < 3):
                wait(act, "YP", j - 2)
            for c in range(2):
                wait(act, "hid", 2 * j + c + 1)
                act.activation(hhi[n % 3][:, 4 * c:4 * c + 4, :].rearrange("p f n -> p (f n)"), HB[n % 2][:, c, :],
                               ACT.Relu).then_inc(sem("hhi"), 1)

        def weigh(j, n):
            wait(act, "yb", j + 1)
            wait(act, "wv", j + 1)
            if not (isinstance(j, int) and j < 2):
                wait(act, "add", 16 * (j - 1))
            act.activation(ysc[n % 2][:, :], yb[:, :], ACT.Copy, scale=wv[n % 6][:, 0:1]).then_inc(sem("ysc"), 1)

        def step(j, n):
            fixed = isinstance(j, int)
            if fixed and j == 0:
                xhalf(0, 0)
            if not (fixed and j < LAG):
                weigh(j - LAG, n - LAG)
            if not (fixed and j >= NBLK - 1):
                xhalf(j + 1, n + 1)
            if not (fixed and j >= NBLK):
                hidden(j, n)

        blocks(step, act)
        for s in range(NS):
            q = s % 2
            act.wait_ge(sem("dev"), s + 1)
            for t in range(4):
                ins = act.activation(X2R[:, 4 * s + t, 0:D], X2R[:, 4 * s + t, 0:D], ACT.Identity,
                                     bias=shift[q][:, t:t + 1], scale=rstd[q][:, t:t + 1])
            ins.then_inc(sem("fin"), 1)

    @block.vector
    def _(dve):
        chain = Chain(dve, sem("dve_chain2"))

        def bc(t):
            return t.unsqueeze(2).to_broadcast([P, NT, NE])

        dve.memset(ones[:, :], 1.0).then_inc(sem("ones_r"), 1)
        dve.wait_ge(sem("ld_route"), 64)
        top, den, rden, w1, w2, best = (small[:, n, :] for n in range(6))
        chain(dve.tensor_reduce(top, LG[:, :, :], AX.X, ALU.max))
        dve.tensor_tensor(eq[:, :, :], LG[:, :, :], bc(top), ALU.subtract).then_inc(sem("centred"), 1)
        dve.wait_ge(sem("ex"), 1)
        chain(dve.tensor_reduce(den, ex[:, :, :], AX.X, ALU.add))
        chain(dve.reciprocal(rden, den))
        chain(dve.tensor_tensor(pr[:, :, :], ex[:, :, :], bc(rden), ALU.mult))
        for k, w in ((0, w1), (1, w2)):
            chain(dve.tensor_reduce(w, pr[:, :, :], AX.X, ALU.max))
            chain(dve.tensor_tensor(eq[:, :, :], pr[:, :, :], bc(w), ALU.is_equal))
            chain(dve.tensor_tensor(eq[:, :, :], eq[:, :, :],
                                    desc[:, :].unsqueeze(1).to_broadcast([P, NT, NE]), ALU.mult))
            chain(dve.tensor_reduce(best, eq[:, :, :], AX.X, ALU.max))
            chain(dve.tensor_tensor(oh[k][:, :, :], eq[:, :, :], bc(best), ALU.is_equal))
            if k == 0:
                chain(dve.tensor_scalar(X2R[:, :, D + 3], best, -1.0, float(NE), ALU.mult, ALU.add))
                chain(dve.tensor_scalar(eq[:, :, :], oh[0][:, :, :], -2.0, None, ALU.mult))
                chain(dve.tensor_tensor(pr[:, :, :], pr[:, :, :], eq[:, :, :], ALU.add))
        chain(dve.tensor_copy(X2R[:, :, D], w1))
        chain(dve.tensor_copy(X2R[:, :, D + 2], ids[:, :]))
        chain(dve.tensor_copy(X2R[:, :, D + 1], w2))
        dve.tensor_tensor(both[:, :, :], oh[0][:, :, :], oh[1][:, :, :], ALU.add).then_inc(sem("both"), 1)
        dve.wait_ge(sem("counts"), 1)
        tot = R1[:, 0:NT * NE].rearrange("p (t e) -> p t e", e=NE)
        for e in range(NE):
            chain.put(dve.tensor_tensor_scan(cum[:, e, :], ones[:, 0:NT], tot[:, :, e], 0.0, ALU.mult, ALU.add))
        chain.wait()
        n, n127, nb, cb, base, _ = (cnt[:, k, :] for k in range(6))
        chain(dve.tensor_copy(n, cum[:, :, NT - 1]))
        chain(dve.tensor_tensor(at[:, :, :], cum[:, :, :].rearrange("p e t -> p t e"), tot, ALU.subtract))
        chain(dve.tensor_tensor(at[:, :, :], at[:, :, :], R0[:, 0:NT * NE].rearrange("p (t e) -> p t e", e=NE),
                                ALU.add))
        chain(dve.tensor_scalar(n127, n, float(P - 1), None, ALU.add))
        chain(dve.tensor_copy(cnti[:, 0, :], n127))
        chain(dve.tensor_scalar(cnti[:, 1, :], cnti[:, 0, :], 7, None, ALU.arith_shift_right))
        chain(dve.tensor_copy(nb, cnti[:, 1, :]))
        chain(dve.tensor_tensor_scan(cb, ones[:, 0:NE], nb, 0.0, ALU.mult, ALU.add))
        chain(dve.tensor_tensor(base, cb, nb, ALU.subtract))
        chain(dve.tensor_scalar(base, base, float(P), None, ALU.mult))
        chain(dve.tensor_tensor(at[:, :, :], at[:, :, :], base.unsqueeze(1).to_broadcast([P, NT, NE]), ALU.add))
        for k in range(2):
            chain(dve.tensor_tensor(eq[:, :, :], at[:, :, :], oh[k][:, :, :], ALU.mult))
            chain(dve.tensor_reduce(pos[:, k, :], eq[:, :, :], AX.X, ALU.add))
        dve.tensor_copy(posu[:, :, :], pos[:, :, :]).then_inc(sem("posu"), 1)
        chain(dve.tensor_tensor(cmp[:, :, :], jrow[:, :].unsqueeze(2).to_broadcast([P, NBLK + 1, NE]),
                                cb.unsqueeze(1).to_broadcast([P, NBLK + 1, NE]), ALU.is_ge))
        chain(dve.tensor_reduce(BEf[:, :], cmp[:, :, :], AX.X, ALU.add))
        chain(dve.tensor_scalar(BEf[:, :], BEf[:, :], float(NE - 1), None, ALU.min))
        def of_rounds(r):
            first = HEAD - 2 + r
            return BEf[:, first:first + ROUND * (ROUNDS - 1) + 1:ROUND]

        for r in range(ROUND, -1, -1):
            chain(dve.scalar_tensor_tensor(PKf[:, 0:ROUNDS], of_rounds(r + 1) if r == ROUND else PKf[:, 0:ROUNDS],
                                           float(NE), of_rounds(r), ALU.mult, ALU.add))
        chain(dve.tensor_copy(PKi[:, 0:ROUNDS], PKf[:, 0:ROUNDS]))
        dve.tensor_copy(BEi[:, :], BEf[:, :]).then_inc(sem("table"), 1)
        dve.wait_ge(sem("table"), 1)

        found, peeled = {}, {}

        def expert(j, n):
            if not isinstance(j, int):
                return (found[n] if n >= HEAD - 2 else
                        dve.value_load(BEi[0:1, bass.ds(j, 1)], min_val=0, max_val=NE - 1))
            if j not in peeled:
                peeled[j] = dve.value_load(BEi[0:1, bass.ds(j, 1)], min_val=0, max_val=NE - 1)
            return peeled[j]

        def xhalf(j, n):
            wait(dve, "xhi", j + 1)
            dve.tensor_tensor(xlo[n % 2][:, :, :], XTp[:, 0:D].rearrange("p (k n) -> p k n", k=KT),
                              xhi[n % 2][:, :, :], ALU.subtract).then_inc(sem("xlo"), 1)

        def hidden(j, n, e, c):
            bank = HB[n % 2][:, c, :].rearrange("p (f n) -> p f n", n=P)
            wait(dve, "HB", 2 * j + c + 1)
            dve.scalar_tensor_tensor(bank, bank, SC[:, 3:4],
                                     b1c[:, bass.ds(e, 1), 4 * c:4 * c + 4].rearrange("p e f -> p (e f)")
                                     .unsqueeze(2).to_broadcast([P, 4, P]), ALU.mult, ALU.add
                                     ).then_inc(sem("hid"), 1)

        def low(j, n, c):
            wait(dve, "hhi", 2 * j + c + 1)
            dve.scalar_tensor_tensor(hlo[n % 3][:, 4 * c:4 * c + 4, :].rearrange("p f n -> p (f n)"),
                                     HB[n % 2][:, c, :], 0.0,
                                     hhi[n % 3][:, 4 * c:4 * c + 4, :].rearrange("p f n -> p (f n)"),
                                     ALU.max, ALU.subtract).then_inc(sem("hlo"), 1)

        def weights(j, n):
            if not (isinstance(j, int) and j < 6):
                wait(dve, "ysc", j - 5)
            wait(dve, "ld_XB", 16 * (j + 1))
            of = BEf[:, bass.ds(j, 1)]
            row = XB[n % 2]
            dve.tensor_scalar(wsel[:, 0:1], row[:, D + 3:D + 4], of, row[:, D:D + 1], ALU.is_equal, ALU.mult)
            chain(dve.tensor_scalar(wsel[:, 1:2], row[:, D + 3:D + 4], of, row[:, D + 1:D + 2],
                                    ALU.not_equal, ALU.mult))
            dve.tensor_tensor(wv[n % 6][:, :], wsel[:, 0:1], wsel[:, 1:2], ALU.add).then_inc(sem("wv"), 1)

        def result(j, n):
            e = expert(j, n)
            wait(dve, "YP", j + 1)
            wait(dve, "ysc", j)
            chain(dve.scalar_tensor_tensor(yl[:, :], YP[n % 2][:, D:2 * D], SC[:, 4:5],
                                           b2r[:, bass.ds(e, 1), :].rearrange("p e d -> p (e d)"),
                                           ALU.mult, ALU.add))
            dve.scalar_tensor_tensor(yb[:, :], YP[n % 2][:, 0:D], SC[:, 4:5], yl[:, :],
                                     ALU.mult, ALU.add).then_inc(sem("yb"), 1)

        def step(j, n):
            fixed = isinstance(j, int)
            now = not (fixed and j >= NBLK)
            if fixed and j == 0:
                dve.wait_ge(sem("ld_b2"), 16)
                xhalf(0, 0)
            if now:
                weights(j, n)
            if not (fixed and j < LAG):
                result(j - LAG, n - LAG)
            if now:
                e = expert(j, n)
                hidden(j, n, e, 0)
            if not (fixed and j >= NBLK - 1):
                xhalf(j + 1, n + 1)
            if now:
                low(j, n, 0)
                hidden(j, n, e, 1)
                low(j, n, 1)

        blocks(step, dve, chain, 2, lambda m: packed(dve, m, found))

        def moments(s):
            q = s % 2
            dve.wait_ge(sem(f"ld_Y{s}"), 16)
            if s >= 2:
                dve.wait_ge(sem("dev"), s - 1)
            if s:
                dve.wait_ge(sem("mom"), s)
            for t in range(4):
                ins = dve.bn_stats(stats[:, t, :], X2R[:, 4 * s + t, 0:D])
            chain(ins)
            for t in range(4):
                ins = dve.bn_aggr(mv[q][:, t, :], stats[:, t, :])
            ins.then_inc(sem("mom"), 1)

        for s in range(NS):
            moments(s)

    @block.gpsimd
    def _(pool):
        chain = Chain(pool, sem("pool_chain2"))
        pool.wait_ge(sem("posu"), 1)
        for t in range(NT):
            for k in range(2):
                pool.indirect_dma_start(XS, bass.IndirectOffsetOnAxis(ap=posu[:, k, t:t + 1], axis=0),
                                        X2R[:, t, :], None).then_inc(sem("scatter"), 16)

        def number(j, n):
            if not (isinstance(j, int) and j < 6):
                wait(pool, "add", 16 * (j - 5))
            wait_apart(pool, "ld_XB", 16 * (j + 1), "posu", 1)
            pool.tensor_copy(tok[n % 6][:, :], XB[n % 2][:, D + 2:D + 3]).then_inc(sem("tok"), 1)

        def add(j, n):
            fixed = isinstance(j, int)
            after, added = (j + 1, 16 * j) if fixed else (nc.snap(j + 1), nc.snap(16 * j))
            pool.wait_ge(sem("posu"), 1)
            pool.wait_ge(sem("ysc"), after)
            pool.wait_ge(sem("tok"), after)
            wait(pool, "add", added)
            pool.indirect_dma_start(YS, bass.IndirectOffsetOnAxis(ap=tok[n % 6][:, 0:1], axis=0),
                                    ysc[n % 2][:, :], None, compute_op=ALU.add).then_inc(sem("add"), 16)

        def step(j, n):
            fixed = isinstance(j, int)
            if not (fixed and j >= NBLK):
                number(j, n)
            if not (fixed and j < LAG):
                add(j - LAG, n - LAG)

        blocks(step, pool)
        for s in range(NS):
            q = s % 2
            pool.wait_ge(sem("mom"), s + 1)
            if s >= 2:
                pool.wait_ge(sem("fin"), s - 1)
            if s:
                pool.wait_ge(sem("dev"), s)
            chain(pool.tensor_scalar(ve[:, :], mv[q][:, :, 1], EPS, None, ALU.add))
            chain(pool.tensor_tensor(rstd[q][:, :], ve[:, :], mhalf[:, :], ALU.pow))
            chain(pool.tensor_tensor(shift[q][:, :], mv[q][:, :, 0], rstd[q][:, :], ALU.mult))
            pool.tensor_scalar(shift[q][:, :], shift[q][:, :], -1.0, None, ALU.mult).then_inc(sem("dev"), 1)


def _bf16_parts(a):
    out = []
    for _ in range(PARTS):
        u = a.astype(np.float32).view(np.uint32).astype(np.uint64)
        r = ((u + 0x7FFF + ((u >> 16) & 1)) & 0xFFFF0000).astype(np.uint32).view(np.float32)
        out.append(r)
        a = a - r
    return out


def _aux(n, bias):
    q = np.zeros((AUX, H, n), np.float32)
    k = np.zeros((AUX, H, n), np.float32)
    q[0:PARTS] = 1.0
    if bias is not None:
        k[0:PARTS] = np.stack(_bf16_parts(bias))
    for a in range(PARTS):
        for h in range(H):
            k[PARTS + GH * a + h % GH, h] = 1.0
    return [(a.view(np.uint32) >> 16).astype(np.uint16) for a in (q, k)]


def kernel(**inputs):
    import concourse.bacc as _bacc
    from concourse.bass_utils import run_bass_kernel_spmd as _run

    g = {k: np.asarray(v) for k, v in inputs.items()}
    order = np.arange(D).reshape(KT, HM, HD).transpose(0, 2, 1).reshape(D)

    def col(b):
        return np.ascontiguousarray(b[order].reshape(KT, P).T)

    slopes = np.power(np.float32(2.0), np.linspace(-4.0, -0.3, H).astype(np.float32)).astype(np.float32)
    alibi = -(slopes[:, None] * np.arange(L, dtype=np.float32)[None, :])
    aux_q, aux_k = _aux(L, alibi)
    aux_cq, _ = _aux(L, None)
    _, aux_ck = _aux(LC, None)
    fill = np.zeros((P, ROW), np.float32)
    fill[:, D + 2] = T + np.arange(P)
    arrays = dict(
        x=g["x"], xT=g["x"].transpose(0, 2, 1), ctxT=g["ctx_1024"].transpose(0, 2, 1),
        mask=g["mask_Bx1x1xS2_fk0"].reshape(B, LC),
        wq=g["L0_attn_Wq"].T[:, order], wk=g["L0_attn_Wk"].T[:, order], wv=g["L0_attn_Wv"].T, wo=g["L0_attn_Wo"].T,
        cwq=g["L0_xattn_Wq"][:, order], cwk=g["L0_xattn_Wk"][:, order], cwv=g["L0_xattn_Wv"], cwo=g["L0_xattn_Wo"],
        bq=col(g["L0_attn_bq"]), bk=col(g["L0_attn_bk"]), cbq=col(g["L0_xattn_bq"]), cbk=col(g["L0_xattn_bk"]),
        bv=g["L0_attn_bv"], bo=g["L0_attn_bo"], cbv=g["L0_xattn_bv"], cbo=g["L0_xattn_bo"],
        gate=g["L0_ffn_gate_w"].T,
        w1=g["L0_ffn_w1"], w2=g["L0_ffn_w2"], b2=g["L0_ffn_b2"],
        b1t=g["L0_ffn_b1"].reshape(NE, FT, P).transpose(2, 0, 1),
        fill=fill, ids=np.arange(T, dtype=np.float32).reshape(NT, P).T,
        tri=np.triu(np.ones((P, P), np.float32), 1),
        desc=np.tile(np.arange(NE, 0, -1, dtype=np.float32), (P, 1)),
        jrow=np.tile(np.arange(NBLK + 1, dtype=np.float32), (P, 1)),
        ident=np.eye(P, dtype=np.float32), aux_q=aux_q, aux_k=aux_k, aux_cq=aux_cq, aux_ck=aux_ck)
    nc = _bacc.Bacc("TRN2", target_bir_lowering=False, num_devices=1)
    feeds, ap = {}, {}
    for name, a in arrays.items():
        a = np.ascontiguousarray(a)
        feeds[f"in_{name}"] = a
        ap[name] = nc.dram_tensor(f"in_{name}", a.shape, mybir.dt.from_np(a.dtype), kind="ExternalInput").ap()
    ap["out"] = nc.dram_tensor("out_y", (T, D), F32, kind="ExternalOutput").ap()
    emit(nc, ap)
    r = _run(nc, [feeds], core_ids=[0])
    return r.results[0]["out_y"].reshape(B, L, D)
```
